# Optimizing a Trainium2 kernel written in Bass

```python
import numpy as np
import jax
import jax.numpy as jnp

def _softmax(x, axis=-1):
    return jax.nn.softmax(x, axis=axis)

def _gelu(x):
    return jax.nn.gelu(x, approximate=True)

def _silu(x):
    return jax.nn.silu(x)

def _sigmoid(x):
    return jax.nn.sigmoid(x)

def _layernorm(x, axis=-1, eps=1e-05):
    m = jnp.mean(x, axis=axis, keepdims=True)
    v = jnp.var(x, axis=axis, keepdims=True)
    return (x - m) / jnp.sqrt(v + eps)

def _scatter_add(tgt, idx, src, axis=0):
    return tgt.at[idx].add(src)

def _segment_sum(src, seg, n):
    return jax.ops.segment_sum(src, seg, n)
kernel_name = 'mk_xattn_ffn_d1_seqx_r8_776fa1'

def setup_inputs(seed: int=0):
    np.random.seed(seed)
    _w = jnp.asarray

    def _rec_inputs():
        import jax
        import jax.numpy as jnp
        _rk = jax.random.key(seed)
        x = 7.22e-05 + 1 * jax.random.normal(jax.random.fold_in(_rk, 1), (16, 128, 256), jnp.float32)
        _lenS = 128 - jax.random.randint(jax.random.fold_in(_rk, 7), (16,), 0, max(1, 128 // 4) + 1, jnp.int32)
        _lenS2 = 128 - jax.random.randint(jax.random.fold_in(_rk, 8), (16,), 0, max(1, 128 // 4) + 1, jnp.int32)
        _ctx_512P = jax.random.normal(jax.random.fold_in(_rk, 11), (16, 16, 64), jnp.float32)
        _ctx_512c = jax.random.dirichlet(jax.random.fold_in(_rk, 511), 0.3 * jnp.ones((16,), jnp.float32), (16, 128))
        _ctx_512t = jnp.einsum('bsk,bkd->bsd', _ctx_512c, _ctx_512P)
        _ctx_512t = _ctx_512t * jax.lax.rsqrt(jnp.mean(jnp.square(_ctx_512t)) + 1e-12) * 0.953939
        ctx_512 = -0.000514642 + 1.00011 * (_ctx_512t + 0.3 * jax.random.normal(jax.random.fold_in(_rk, 611), (16, 128, 64), jnp.float32))
        return (x, ctx_512)
    x, ctx_512 = _rec_inputs()

    def _L0_xattn_setup():
        import jax, jax.numpy as jnp
        import numpy as np
        import math
        NUM_Q_HEADS = 32
        NUM_KV_HEADS = 8
        key = jax.random.key(seed)
        k1, k2, k3 = jax.random.split(key, 3)
        B, S, E = (2, 256, 256)
        kv_E = NUM_KV_HEADS * (E // NUM_Q_HEADS)
        q = jax.random.normal(k1, (B, S, E), dtype=jnp.float32)
        k = jax.random.normal(k2, (B, S, kv_E), dtype=jnp.float32)
        v = jax.random.normal(k3, (B, S, kv_E), dtype=jnp.float32)
        return {'q': q, 'k': k, 'v': v}
    _L0_xattn_all = _L0_xattn_setup()
    _L0_xattn_in = {k: v for k, v in _L0_xattn_all.items() if k in ()}
    del _L0_xattn_all

    def _L0_ffn_setup():
        import jax, jax.numpy as jnp
        import numpy as np
        NUM_ACT = 2
        key = jax.random.key(seed)
        k1, k2, k3, k4, k5 = jax.random.split(key, 5)
        B, S, D, I, E = (4, 64, 256, 512, 8)
        x = jax.random.normal(k1, (B, S, D), dtype=jnp.float32)
        gate_w = jax.random.normal(k2, (E, D), dtype=jnp.float32) * 0.02
        w1 = jax.random.normal(k3, (E, I, D), dtype=jnp.float32) * 0.02
        w2 = jax.random.normal(k4, (E, D, I), dtype=jnp.float32) * 0.02
        w3 = jax.random.normal(k5, (E, I, D), dtype=jnp.float32) * 0.02
        return {'x': x, 'gate_w': gate_w, 'w1': w1, 'w2': w2, 'w3': w3}
    _L0_ffn_all = _L0_ffn_setup()
    _L0_ffn_in = {k: v for k, v in _L0_ffn_all.items() if k in ('gate_w', 'w1', 'w2', 'w3')}
    del _L0_ffn_all
    return {'x': x, 'ctx_512': ctx_512, 'L0_ffn_gate_w': _L0_ffn_in['gate_w'], 'L0_ffn_w1': _L0_ffn_in['w1'], 'L0_ffn_w2': _L0_ffn_in['w2'], 'L0_ffn_w3': _L0_ffn_in['w3']}

def reference(x, ctx_512, L0_ffn_gate_w, L0_ffn_w1, L0_ffn_w2, L0_ffn_w3):
    import jax
    import jax.numpy as jnp

    def _L0_xattn_ref(q, k, v):
        import jax, jax.numpy as jnp
        import numpy as np
        import math
        NUM_Q_HEADS = 32
        NUM_KV_HEADS = 8
        B, S, E = q.shape
        H, KV = (NUM_Q_HEADS, NUM_KV_HEADS)
        D = E // H
        G = H // KV
        scale = math.sqrt(D)
        qh = q.reshape(B, S, KV, G, D).transpose(0, 2, 3, 1, 4)
        kh = k.reshape(B, S, KV, D).transpose(0, 2, 1, 3)
        vh = v.reshape(B, S, KV, D).transpose(0, 2, 1, 3)
        scores = jnp.einsum('bkgsd,bktd->bkgst', qh, kh) / scale
        weights = jax.nn.softmax(scores, axis=-1)
        out = jnp.einsum('bkgst,bktd->bkgsd', weights, vh)
        return out.transpose(0, 3, 1, 2, 4).reshape(B, S, E)

    def _L0_ffn_ref(x, gate_w, w1, w2, w3):
        import jax, jax.numpy as jnp
        import numpy as np
        NUM_ACT = 2
        B, S, D = x.shape
        xt = x.reshape(-1, D)
        scores = jnp.einsum('ti,ei->te', xt, gate_w)
        probs = jax.nn.softmax(scores, axis=-1)
        expert_weights, expert_indices = jax.lax.top_k(probs, NUM_ACT)
        expert_weights = expert_weights / expert_weights.sum(axis=-1, keepdims=True)
        x1 = jax.nn.silu(jnp.einsum('ti,eoi->teo', xt, w1))
        x3 = jnp.einsum('ti,eoi->teo', xt, w3)
        expert_outs_all = jnp.einsum('teo,eio->tei', x1 * x3, w2)
        sel = jnp.take_along_axis(expert_outs_all, expert_indices[:, :, None], axis=1)
        out = jnp.einsum('tai,ta->ti', sel, expert_weights)
        return out.reshape(B, S, D)
    x = x + _L0_xattn_ref(_layernorm(x, axis=-1), ctx_512, ctx_512)
    x = x + _L0_ffn_ref(_layernorm(x, axis=-1), L0_ffn_gate_w, L0_ffn_w1, L0_ffn_w2, L0_ffn_w3)
    return x

_drawn_inputs = setup_inputs


def setup_inputs(seed=0):
    import zlib

    import numpy as np

    out = dict(_drawn_inputs(seed))
    spreads = {}
    factors = {'L0_ffn_gate_w': 5.254, 'L0_ffn_w1': 4.615, 'L0_ffn_w2': 4.568, 'L0_ffn_w3': 4.567}
    for name, (base, spread) in spreads.items():
        noise = np.random.default_rng([zlib.crc32(name.encode()), seed]).standard_normal(out[name].shape)
        drawn = base * np.exp(spread * noise) if base else spread * noise
        out[name] = jnp.asarray(drawn.astype(out[name].dtype))
    for name, factor in factors.items():
        out[name] = (out[name] * factor).astype(out[name].dtype)
    return out
```

```python
from contextlib import ExitStack

import concourse.bass as bass
from concourse import mybir
from concourse.bass import IndirectOffsetOnAxis

ALU = mybir.AluOpType
ACT = mybir.ActivationFunctionType
AX = mybir.AxisListType
F32 = mybir.dt.float32
BF16 = mybir.dt.bfloat16
I32 = mybir.dt.int32
U32 = mybir.dt.uint32

P = 128
B, D, KV, G, HD = 16, 256, 8, 4, 8
H = KV * G
T = B * P
E, F, TOPK = 8, 512, 2
KC, FC = D // P, F // P
EPS = 1e-5
SCALE = 1.0 / float(HD) ** 0.5

TERMS = [(0, 0), (0, 1), (0, 2), (1, 0), (1, 1), (2, 0)]
QK_ROWS = len(TERMS) * HD
QKM_ROWS = QK_ROWS + 3
VW = HD + 1
OT = KV * VW

REGION = T + P
RW = D + 2
NT = (TOPK * T + E * (P - 1)) // P

C_ID, C_TRI, C_ONE, C_IOTA, C_BASE, C_TILE, C_END = 0, 128, 256, 384, 392, 400, 400 + NT


def constants():
    import numpy as np
    c = np.zeros((P, C_END), np.float32)
    p = np.arange(P)
    c[:, C_ID:C_ID + P] = np.eye(P)
    c[:, C_TRI:C_TRI + P] = p[:, None] < p[None, :]
    c[:, C_ONE:C_ONE + P] = 1.0
    c[:, C_IOTA:C_IOTA + E] = np.arange(E)
    c[:, C_BASE:C_BASE + E] = np.arange(E) * REGION
    c[:, C_TILE:C_TILE + NT] = np.arange(NT)
    i = (np.arange(B + 1)[None, :] * P + p[:, None]).astype(np.int32)
    return c, i


def build(nc, x, kT, v, gateT, w1T, w3T, w2T, cf, ci, out):
    kparts_d = nc.dram_tensor("kparts_d", (3, P, KV * P), BF16, kind="Internal").ap()
    qparts_d = nc.dram_tensor("qparts_d", (B, P, 3, KC, P), BF16, kind="Internal").ap()
    slots_d = nc.dram_tensor("slots_d", (E * REGION + P, RW), F32, kind="Internal").ap()

    with ExitStack() as ctx:
        def sb(name, shape, dt=F32):
            return ctx.enter_context(nc.sbuf_tensor(name, shape, dt))

        def sem(name):
            return ctx.enter_context(nc.semaphore(name))

        def sems(name, n):
            return [sem(f"{name}{i}") for i in range(n)]

        w13 = sb("w13", [P, 2, E * KC * F])
        w2 = sb("w2", [P, E * FC * D])
        gate = sb("gate", [P, KC, E])
        cst = sb("cst", [P, C_END])
        tok_id = sb("tok_id", [P, B + 1], I32)
        ident = cst[:, C_ID:C_ID + P]
        identb = sb("identb", [P, P], BF16)
        trib = sb("trib", [P, P], BF16)
        onesb = sb("onesb", [P, P], BF16)
        kst = sb("kst", [64, B, KV * P], BF16)
        vnat = sb("vnat", [P, B, KV, HD])
        vblk = sb("vblk", [P, 2, KV * (OT + VW)])
        arena = sb("arena", [P, 3 * H * P // 2])
        qst = arena[:, :].bitcast(BF16).rearrange("p (r h s) -> p r h s", r=3, h=H)
        prob = sb("prob", [P, 4, G * P])
        xin = sb("xin", [P, 2, D])
        xn1 = sb("xn1", [P, 2, D])
        qp = sb("qp", [P, 2, 3, D], BF16)
        qres = sb("qres", [P, 2, D])
        negm = sb("negm", [P, 2, H])
        negp = sb("negp", [P, 2, 3, H], BF16)
        negr = sb("negr", [P, 2, H])
        negT = sb("negT", [3 * H, 2, P], BF16)
        oT = sb("oT", [OT, 2, G * P])
        rden = sb("rden", [P, H])
        att = sb("att", [P, 2, D])
        xres = sb("xres", [P, 2, D])
        x2 = sb("x2", [P, 2, D])
        stat = sb("stat", [P, 2, 8])
        mv = sb("mv", [P, 2, 2])
        rs = sb("rs", [P, 2, 4])
        rows = sb("rows", [P, 2, TOPK, RW])
        xn2T = sb("xn2T", [P, 2, KC, P])
        lg = sb("lg", [P, E])
        top = sb("top", [P, 8])
        topi = sb("topi", [P, 8], U32)
        topf = sb("topf", [P, TOPK])
        hot = sb("hot", [P, 2, TOPK, E])
        hotb = sb("hotb", [P, 2, E], BF16)
        seen = sb("seen", [P, 2, E], BF16)
        dlt = sb("dlt", [P, 4])
        pos = sb("pos", [P, E])
        posk = sb("posk", [P, TOPK, E])
        slot = sb("slot", [P, 2, TOPK], I32)
        kin = arena[:, 0:1024]
        kres = arena[:, 1024:2048]
        kp = arena[:, 2048:2048 + 1536].bitcast(BF16).rearrange("p (j n) -> p j n", j=3)
        cnt = sb("cnt", [P, E])
        cnti = sb("cnti", [P, 2, E], I32)
        ntl = sb("ntl", [P, E])
        cum = sb("cum", [P, E])
        ge = sb("ge", [P, NT, E])
        gn = sb("gn", [P, NT, E])
        te = sb("te", [P, NT])
        tx = sb("tx", [P, NT])
        ta = sb("ta", [P, NT])
        row0 = sb("row0", [P, NT], I32)
        texp = sb("texp", [P, NT], I32)
        dst = sb("dst", [P, E], I32)
        pad = sb("pad", [P, RW])
        at = 0

        def part(n):
            nonlocal at
            at += n
            return arena[:, at - n:at]

        xs = part(2 * RW).rearrange("p (u c) -> p u c", u=2)
        xT = part(2 * D).rearrange("p (u k s) -> p u k s", u=2, k=KC)
        sil = part(F)
        gat = part(2 * F).rearrange("p (u f) -> p u f", u=2)
        gT = part(F).rearrange("p (c s) -> p c s", c=FC)
        ys = part(2 * D).rearrange("p (u c) -> p u c", u=2)
        meta = part(4).rearrange("p (u c) -> p u c", u=2)

        bank = [ctx.enter_context(nc.psum_tensor(f"bank{i}", [P, 512], F32)) for i in range(8)]
        ps_s = bank[0:2]
        ps_e = bank[2:4]
        ps_o = bank[4:6]
        ps_a, ps_b = bank[6], bank[7]
        ps_h1, ps_h3 = bank[0:2], bank[2:4]
        ps_g, ps_y, ps_x = bank[4], bank[5], bank[6]

        in_const, in_k, in_v, in_w = sem("in_const"), sem("in_k"), sem("in_v"), sem("in_w")
        in_x, in_res = sems("in_x", 2), sems("in_res", 2)
        kparts_out, kst_in = sem("kparts_out"), sem("kst_in")
        qparts_out, qst_in = sems("qparts_out", 2), sems("qst_in", 3)
        neg_in = sems("neg_in", 3)
        x2_out, rows_out = sems("x2_out", 2), sems("rows_out", 2)
        pad_row, pads_out = sem("pad_row"), sem("pads_out")
        const_b, ones_k, k_split = sem("const_b"), sem("ones_k"), sem("k_split")
        v_zero, v_ready = sem("v_zero"), sem("v_ready")
        ln1, ln2, root1, root2 = sem("ln1"), sem("ln2"), sem("root1"), sem("root2")
        qT_ready, q_part, q_res = sem("qT_ready"), sem("q_part"), sem("q_res")
        s_ready, max_done = sem("s_ready"), sem("max_done")
        neg_step, negT_ready, negT_read = sem("neg_step"), sem("negT_ready"), sem("negT_read")
        e_ready, exp_done, pv_done = sem("e_ready"), sem("exp_done"), sem("pv_done")
        oT_read, y_ready, y_step = sem("oT_read"), sem("y_ready"), sem("y_step")
        x2_ready, row_copied, tok_put = sem("x2_ready"), sem("row_copied"), sem("tok_put")
        xT2_ready, xT2_read, lg_ready, route = sem("xT2_ready"), sem("xT2_read"), sem("lg_ready"), sem("route")
        w_exp, w_step, hot_done = sem("w_exp"), sem("w_step"), sem("hot_done")
        seen_ready, rank_ready, pos_step = sem("seen_ready"), sem("rank_ready"), sem("pos_step")
        cnt_ready, table = sem("cnt_ready"), sem("table")
        xs_in = sems("xs_in", 2)
        xT_ready, xT_read, h1_ready, h3_ready = sem("xT_ready"), sem("xT_read"), sem("h1_ready"), sem("h3_ready")
        sil_done, g_done, gT_ready, gT_read = sem("sil_done"), sem("g_done"), sem("gT_ready"), sem("gT_read")
        y2_ready, y2_read, meta_done, added = sem("y2_ready"), sem("y2_read"), sem("meta_done"), sems("added", 2)

        LN, ROOT, ROUTE, POS, TABLE = 5, 8, 6, 3, 14
        S_AT = [3, 3, 2, 0, 0, 0, 0, 0]

        block = ctx.enter_context(nc.Block())

        @block.sync
        def _(sp):
            sp.dma_start(kin, kT).then_inc(in_k, 16)
            for b in range(2):
                sp.dma_start(xin[:, b, :], x[b * P:(b + 1) * P, :]).then_inc(in_x[b], 16)
            sp.dma_start(cst[:, :], cf).then_inc(in_const, 16)
            sp.dma_start(tok_id[:, :], ci).then_inc(in_const, 16)
            sp.dma_start(gate[:, :, :], gateT).then_inc(in_const, 16)
            sp.dma_start(vnat[:, :, :, :], v.rearrange("(b t) (k d) -> t b k d", t=P, k=KV)).then_inc(in_v, 16)
            sp.wait_ge(k_split, 4)
            sp.dma_start(kparts_d.rearrange("j p n -> p j n"), kp).then_inc(kparts_out, 16)
            sp.wait_ge(kparts_out, 16)
            sp.wait_ge(ones_k, 1)
            kd = kparts_d.rearrange("j (b d) n -> j d b n", d=HD)
            for i, (_, j) in enumerate(TERMS):
                sp.dma_start(kst[i * HD:(i + 1) * HD, :, :], kd[j]).then_inc(kst_in, 16)

            def load_x(b):
                sp.wait_ge(ln1, LN * (b - 1))
                sp.dma_start(xin[:, b % 2, :], x[b * P:(b + 1) * P, :]).then_inc(in_x[b % 2], 16)

            def load_res(b):
                if b >= 2:
                    sp.wait_ge(x2_ready, b - 1)
                sp.dma_start(xres[:, b % 2, :], x[b * P:(b + 1) * P, :]).then_inc(in_res[b % 2], 16)

            def store_x2(b):
                sp.wait_ge(x2_ready, b + 1)
                sp.dma_start(out[b * P:(b + 1) * P, :], x2[:, b % 2, :]).then_inc(x2_out[b % 2], 16)

            def stack_q(b):
                sp.wait_ge(q_res, 2 * b + 2)
                sp.dma_start(qparts_d[b], qp[:, b % 2].rearrange("p j (c s) -> p j c s", c=KC))\
                    .then_inc(qparts_out[b % 2], 16)
                sp.wait_ge(qparts_out[b % 2], 16 * (b // 2 + 1))
                if b >= 3:
                    sp.wait_ge(e_ready, 8 * (b - 2))
                if b == 0:
                    sp.wait_ge(kparts_out, 16)
                qd = qparts_d[b].rearrange("(h d) j c s -> j d c h s", d=HD)
                for i, (j, _) in enumerate(TERMS):
                    for c in range(KC):
                        sp.dma_start(qst[i * HD:(i + 1) * HD, b % 3, c * (H // KC):(c + 1) * (H // KC), :],
                                     qd[j, :, c]).then_inc(qst_in[b % 3], 16)

            def load_weights(e):
                n, m = KC * F, FC * D
                sp.dma_start(w13[:, 0, e * n:(e + 1) * n], w1T[:, e * n:(e + 1) * n]).then_inc(in_w, 16)
                sp.dma_start(w13[:, 1, e * n:(e + 1) * n], w3T[:, e * n:(e + 1) * n]).then_inc(in_w, 16)
                sp.dma_start(w2[:, e * m:(e + 1) * m], w2T[:, e * m:(e + 1) * m]).then_inc(in_w, 16)

            for i in range(-3, B + 1):
                if 2 <= i + 4 < B:
                    load_x(i + 4)
                if 0 <= i < B:
                    load_res(i)
                if 0 <= i + 2 < B:
                    stack_q(i + 2)
                if 1 <= i <= E:
                    load_weights(i - 1)
                if 0 <= i - 1 < B:
                    store_x2(i - 1)

            sp.wait_ge(pad_row, 3)
            sp.dma_start(out[T:T + P, :], pad[:, 0:D]).then_inc(pads_out, 16)
            sp.dma_start(slots_d[E * REGION:E * REGION + P, :], pad[:, :]).then_inc(pads_out, 16)
            sp.wait_ge(table, TABLE)
            for e in range(E):
                r = sp.value_load(dst[0:1, e:e + 1], min_val=e * REGION, max_val=e * REGION + T)
                sp.dma_start(slots_d[bass.ds(r, P), :], pad[:, :]).then_inc(pads_out, 16)
            sp.wait_ge(pads_out, 16 * (E + 2))
            for u in range(2):
                sp.wait_ge(rows_out[u], 16 * B)
                sp.wait_ge(x2_out[u], 16 * B // 2)

            def load_tile(j, u):
                r = sp.value_load(row0[0:1, bass.ds(j, 1)], min_val=0, max_val=E * REGION)
                if not (isinstance(j, int) and j < 2):
                    sp.wait_ge(xT_ready, j - 1)
                    sp.wait_ge(meta_done, j - 1)
                sp.dma_start(xs[:, u, :], slots_d[bass.ds(r, P), :]).then_inc(xs_in[u], 16)

            for j in range(NT):
                load_tile(j, j % 2)

        @block.gpsimd
        def _(pool):
            pool.memset(vblk[:, :, :], 0.0).then_inc(v_zero, 1)
            pool.memset(seen[:, 0, :], 0.0).then_inc(seen_ready, 1)
            pool.wait_ge(v_zero, 1)
            vb = vblk[:, :, :].rearrange("p u (k r) -> p u k r", k=KV)
            for u in range(2):
                pool.memset(vb[:, u, :, HD:HD + 1], 1.0).then_inc(v_zero, 1)
            pool.memset(pad[:, :], 0.0).then_inc(pad_row, 1)
            pool.wait_ge(pad_row, 1)
            pool.wait_ge(in_const, 48)
            pool.tensor_copy(pad[:, D:D + 1].bitcast(I32), tok_id[:, B:B + 1]).then_inc(pad_row, 2)
            pool.wait_ge(in_v, 16)
            pool.wait_ge(v_zero, 3)

            def put_v(b):
                if b >= 2:
                    pool.wait_ge(pv_done, 8 * (b - 1))
                pool.tensor_copy(vb[:, b % 2, :, 0:HD], vnat[:, b]).then_inc(v_ready, 1)

            def add_res(b):
                pool.wait_ge(y_step, 2 * b + 2)
                pool.wait_ge(in_res[b % 2], 16 * (b // 2 + 1))
                if b >= 2:
                    pool.wait_ge(x2_out[b % 2], 16 * (b // 2))
                    pool.wait_ge(ln2, LN * (b - 1))
                pool.tensor_tensor(x2[:, b % 2, :], att[:, b % 2, :], xres[:, b % 2, :], ALU.add)\
                    .then_inc(x2_ready, 1)
                if b >= 2:
                    pool.wait_ge(rows_out[b % 2], 32 * (b // 2))
                for k in range(TOPK):
                    pool.tensor_copy(rows[:, b % 2, k, D:D + 1].bitcast(I32), tok_id[:, b:b + 1])\
                        .then_inc(tok_put, 1)

            def copy_row(b):
                pool.wait_ge(ln2, LN * b + LN)
                pool.tensor_copy(rows[:, b % 2, 1, 0:D], rows[:, b % 2, 0, 0:D]).then_inc(row_copied, 1)

            def add_seen(b):
                pool.wait_ge(route, ROUTE * b + 6)
                pool.wait_ge(seen_ready, b + 1)
                if b >= 1:
                    pool.wait_ge(rank_ready, b)
                pool.tensor_tensor(seen[:, (b + 1) % 2, :], seen[:, b % 2, :], hotb[:, b % 2, :], ALU.add)\
                    .then_inc(seen_ready, 1)

            def scatter(b):
                pool.wait_ge(pos_step, POS * b + 3)
                pool.wait_ge(row_copied, b + 1)
                pool.wait_ge(w_step, 3 * b + 3)
                pool.wait_ge(tok_put, 2 * b + 2)
                for k in range(TOPK):
                    pool.indirect_dma_start(
                        slots_d, IndirectOffsetOnAxis(ap=slot[:, b % 2, k:k + 1], axis=0),
                        rows[:, b % 2, k, :], None).then_inc(rows_out[b % 2], 16)

            def root(n, b, guessed, done):
                v, y, h, p = (rs[:, n, c:c + 1] for c in range(4))
                pool.wait_ge(guessed, LN * b + 4)
                for r in range(0, ROOT, 4):
                    pool.tensor_scalar(h, y, y, v, ALU.mult, ALU.mult).then_inc(done, 1)
                    pool.wait_ge(done, ROOT * b + r + 1)
                    pool.tensor_scalar(p, h, 3 / 8, -10 / 8, ALU.mult, ALU.add).then_inc(done, 1)
                    pool.wait_ge(done, ROOT * b + r + 2)
                    pool.tensor_scalar(p, p, h, 15 / 8, ALU.mult, ALU.add).then_inc(done, 1)
                    pool.wait_ge(done, ROOT * b + r + 3)
                    pool.tensor_tensor(y, y, p, ALU.mult).then_inc(done, 1)
                    if r + 4 < ROOT:
                        pool.wait_ge(done, ROOT * b + r + 4)

            root(0, 0, ln1, root1)
            for i in range(-2, B + 2):
                if 0 <= i + 1 < B:
                    put_v(i + 1)
                if 0 <= i - 1 < B:
                    add_res(i - 1)
                    root(1, i - 1, ln2, root2)
                if 0 <= i + 3 < B:
                    root(0, i + 3, ln1, root1)
                if 0 <= i - 2 < B:
                    scatter(i - 2)
                if 0 <= i - 1 < B:
                    copy_row(i - 1)
                    add_seen(i - 1)

            pool.wait_ge(pads_out, 16 * (E + 2))
            for u in range(2):
                pool.wait_ge(x2_out[u], 16 * B // 2)

            def add_out(j, u):
                pool.wait_ge(y2_read, j + 1)
                pool.wait_ge(meta_done, j + 1)
                pool.indirect_dma_start(
                    out, IndirectOffsetOnAxis(ap=meta[:, u, 0:1].bitcast(I32), axis=0),
                    ys[:, u, :], None, compute_op=ALU.add).then_inc(added[u], 16)
                pool.wait_ge(added[u], 16 * (j // 2 + 1))

            for j in range(NT):
                add_out(j, j % 2)

        @block.tensor
        def _(pe):
            pe.wait_ge(in_const, 48)
            pe.wait_ge(const_b, 3)

            def q_transpose(b):
                pe.wait_ge(ln1, LN * b + LN)
                if b >= 2:
                    pe.wait_ge(negT_read, b - 1)
                elif b == 1:
                    pe.wait_ge(q_res, 1)
                for c in range(KC):
                    m = pe.transpose(ps_a[:, c * P:(c + 1) * P], xn1[:, b % 2, c * P:(c + 1) * P], ident)
                m.then_inc(qT_ready, 1)

            def score_group(b, g):
                if g == 0:
                    pe.wait_ge(qst_in[b % 3], 16 * len(TERMS) * KC * (b // 3 + 1))
                    if b == 0:
                        pe.wait_ge(kst_in, 16 * len(TERMS))
                if 8 * b + g >= 2:
                    pe.wait_ge(max_done, 8 * b + g - 1)
                for h in range(G * g, G * g + G):
                    m = pe.matmul(ps_s[g % 2][:, (h % G) * P:(h % G + 1) * P], qst[0:QK_ROWS, b % 3, h, :],
                                  kst[0:QK_ROWS, b, g * P:(g + 1) * P], start=True, stop=True)
                m.then_inc(s_ready, 1)

            def neg_transpose(b):
                pe.wait_ge(neg_step, 4 * b + 4)
                if b >= 3:
                    pe.wait_ge(pos_step, POS * (b - 3) + 1)
                if b + 1 < B:
                    pe.wait_ge(q_res, 2 * (b + 1) + 1)
                pe.transpose(ps_a[0:3 * H, 0:P // 2].bitcast(BF16), negp[:, b % 2].rearrange("p j h -> p (j h)"),
                             identb[:, :]).then_inc(negT_ready, 1)

            def e_products(b, k):
                if k == 0:
                    pe.wait_ge(neg_in[b % 3], 48 * (b // 3 + 1))
                if 8 * b + k >= 2:
                    pe.wait_ge(exp_done, 8 * b + k - 1)
                pe.matmul(ps_e[k % 2][:, :], kst[0:QKM_ROWS, b, k * P:(k + 1) * P],
                          qst[0:QKM_ROWS, b % 3, k * G:(k + 1) * G, :].rearrange("p h s -> p (h s)"),
                          start=True, stop=True).then_inc(e_ready, 1)

            def pv(b, k):
                if k == 0:
                    pe.wait_ge(v_ready, b + 1)
                    if b >= 2:
                        pe.wait_ge(oT_read, b - 1)
                pe.wait_ge(exp_done, 8 * b + k + 1)
                pe.matmul(ps_o[b % 2][0:OT, :], vblk[:, b % 2, k * OT:(k + 1) * OT], prob[:, k % 4, :],
                          start=(k == 0), stop=(k == KV - 1)).then_inc(pv_done, 1)

            def y_transpose(b):
                pe.wait_ge(oT_read, b + 1)
                if b >= 1:
                    pe.wait_ge(route, ROUTE * (b - 1) + 1)
                for g in range(G):
                    m = pe.transpose(ps_b[:, g * OT:(g + 1) * OT], oT[:, b % 2, g * P:(g + 1) * P],
                                     ident[0:OT, 0:OT])
                m.then_inc(y_ready, 1)

            def x2_transpose(b):
                pe.wait_ge(ln2, LN * b + LN)
                pe.wait_ge(y_step, 2 * b + 2)
                for c in range(KC):
                    m = pe.transpose(ps_b[:, c * P:(c + 1) * P], rows[:, b % 2, 0, c * P:(c + 1) * P], ident)
                m.then_inc(xT2_ready, 1)

            def logits(b):
                pe.wait_ge(xT2_read, b + 1)
                for c in range(KC):
                    m = pe.matmul(ps_b[:, 0:E], xn2T[:, b % 2, c, :], gate[:, c, :],
                                  start=(c == 0), stop=(c == KC - 1))
                m.then_inc(lg_ready, 1)

            def ranks(b):
                pe.wait_ge(route, ROUTE * b + 6)
                pe.wait_ge(seen_ready, b + 1)
                if b + 4 < B:
                    pe.wait_ge(q_res, 2 * (b + 4) + 1)
                else:
                    pe.wait_ge(negT_read, min(b + 3, B))
                pe.matmul(ps_a[:, 0:E], trib[:, :], hotb[:, b % 2, :], start=True, stop=False)
                pe.matmul(ps_a[:, 0:E], onesb[:, :], seen[:, b % 2, :], start=False, stop=True)\
                    .then_inc(rank_ready, 1)

            for i in range(-2, B + 2):
                for k in range(KV):
                    if 0 <= i < B:
                        e_products(i, k)
                    if k == 0 and 0 <= i - 1 < B:
                        pv(i - 1, KV - 1)
                    if k == 1 and 0 <= i + 2 < B:
                        q_transpose(i + 2)
                    if k == 2 and 0 <= i - 1 < B:
                        y_transpose(i - 1)
                    if 0 <= i + 1 < B:
                        for g in range(sum(S_AT[:k]), sum(S_AT[:k + 1])):
                            score_group(i + 1, g)
                    if k == 3 and 0 <= i - 2 < B:
                        ranks(i - 2)
                    if k == 5 and 0 <= i - 1 < B:
                        x2_transpose(i - 1)
                    if k == 6 and 0 <= i + 1 < B:
                        neg_transpose(i + 1)
                    if k == 7 and 0 <= i - 1 < B:
                        logits(i - 1)
                    if k >= 1 and 0 <= i < B:
                        pv(i, k - 1)
            pe.wait_ge(seen_ready, B + 1)
            pe.wait_ge(pos_step, POS * B)
            pe.matmul(ps_a[:, 0:E], onesb[:, :], seen[:, B % 2, :], start=True, stop=True).then_inc(cnt_ready, 1)

            pe.wait_ge(table, TABLE)
            pe.wait_ge(in_w, 16 * 3 * E)

            def tile_transpose(j, u):
                pe.wait_ge(xs_in[u], 16 * (j // 2 + 1) if isinstance(j, int) else (j - u) * 8 + 16)
                if not (isinstance(j, int) and j < 1):
                    pe.wait_ge(xT_read, j)
                for c in range(KC):
                    m = pe.transpose(ps_x[:, c * P:(c + 1) * P], xs[:, u, c * P:(c + 1) * P], ident)
                m.then_inc(xT_ready, 1)

            def tile_h(j, u, w, e, bank_, done, used):
                pe.wait_ge(xT_read, j + 1)
                if not (isinstance(j, int) and j < 2):
                    pe.wait_ge(used, j - 1)
                for c in range(KC):
                    m = pe.matmul(bank_[u][:, :], xT[:, u, c, :],
                                  w13[:, w, bass.ds(e * (KC * F) + c * F, F)], start=(c == 0), stop=(c == KC - 1))
                m.then_inc(done, 1)

            def g_transpose(j, u):
                pe.wait_ge(g_done, j + 1)
                if not (isinstance(j, int) and j < 1):
                    pe.wait_ge(gT_read, j)
                for c in range(FC):
                    m = pe.transpose(ps_g[:, c * P:(c + 1) * P], gat[:, u, c * P:(c + 1) * P], ident)
                m.then_inc(gT_ready, 1)

            def tile_y(j, u, e):
                pe.wait_ge(gT_read, j + 1)
                if not (isinstance(j, int) and j < 1):
                    pe.wait_ge(y2_read, j)
                for c in range(FC):
                    m = pe.matmul(ps_y[:, 0:D], gT[:, c, :], w2[:, bass.ds(e * (FC * D) + c * D, D)],
                                  start=(c == 0), stop=(c == FC - 1))
                m.then_inc(y2_ready, 1)

            def expert(j):
                return pe.value_load(texp[0:1, bass.ds(j, 1)], min_val=0, max_val=E - 1)

            tile_transpose(0, 0)
            last = None
            for j in range(NT):
                e = expert(j)
                tile_h(j, j % 2, 0, e, ps_h1, h1_ready, sil_done)
                if j > 0:
                    g_transpose(j - 1, (j - 1) % 2)
                tile_h(j, j % 2, 1, e, ps_h3, h3_ready, g_done)
                if j + 1 < NT:
                    tile_transpose(j + 1, (j + 1) % 2)
                if j > 0:
                    tile_y(j - 1, (j - 1) % 2, last)
                last = e
            g_transpose(NT - 1, (NT - 1) % 2)
            tile_y(NT - 1, (NT - 1) % 2, last)

        @block.scalar
        def _(act):
            def exps(b, k):
                n = 8 * b + k
                act.wait_ge(e_ready, n + 1)
                if n >= 4:
                    act.wait_ge(pv_done, n - 3)
                act.activation(prob[:, k % 4, :], ps_e[k % 2][:, :], ACT.Exp, scale=SCALE).then_inc(exp_done, 1)

            def q_part1(b):
                act.wait_ge(qT_ready, b + 1)
                if b >= 2:
                    act.wait_ge(qparts_out[b % 2], 16 * (b // 2))
                act.activation(qp[:, b % 2, 0, :], ps_a[:, 0:D], ACT.Copy).then_inc(q_part, 1)

            def q_part2(b):
                act.wait_ge(q_res, 2 * b + 1)
                act.activation(qp[:, b % 2, 1, :], qres[:, b % 2, :], ACT.Copy).then_inc(q_part, 1)

            def copy_oT(b):
                act.wait_ge(pv_done, 8 * b + 8)
                if b >= 2:
                    act.wait_ge(y_ready, b - 1)
                act.activation(oT[:, b % 2, :], ps_o[b % 2][0:OT, :], ACT.Copy).then_inc(oT_read, 1)

            def copy_x2T(b):
                act.wait_ge(xT2_ready, b + 1)
                if b >= 2:
                    act.wait_ge(lg_ready, b - 1)
                act.activation(xn2T[:, b % 2].rearrange("p c s -> p (c s)"), ps_b[:, 0:D], ACT.Copy)\
                    .then_inc(xT2_read, 1)

            def copy_negT(b):
                act.wait_ge(negT_ready, b + 1)
                if b >= 2:
                    act.wait_ge(neg_in[(b - 2) % 3], 48 * ((b - 2) // 3 + 1))
                act.activation(negT[:, b % 2, :], ps_a[0:3 * H, 0:P // 2].bitcast(BF16), ACT.Copy)\
                    .then_inc(negT_read, 1)
                act.wait_ge(negT_read, b + 1)
                if b >= 3:
                    act.wait_ge(e_ready, 8 * (b - 2))
                for j in range(3):
                    act.dma_start(qst[QK_ROWS + j:QK_ROWS + j + 1, b % 3, :, :],
                                  negT[j * H:(j + 1) * H, b % 2, :]).then_inc(neg_in[b % 3], 16)

            def weight_exp(b):
                act.wait_ge(route, ROUTE * b + 3)
                if b >= 1:
                    act.wait_ge(w_step, 3 * b)
                act.activation(dlt[:, 1:2], dlt[:, 0:1], ACT.Exp).then_inc(w_exp, 1)

            for i in range(-2, B + 1):
                for k in range(KV):
                    if 0 <= i < B:
                        exps(i, k)
                    if k == 0 and 0 <= i - 1 < B:
                        copy_oT(i - 1)
                    if k == 1 and 0 <= i + 2 < B:
                        q_part1(i + 2)
                    if k == 3 and 0 <= i + 2 < B:
                        q_part2(i + 2)
                    if k == 5 and 0 <= i - 1 < B:
                        copy_x2T(i - 1)
                    if k == 6 and 0 <= i + 1 < B:
                        copy_negT(i + 1)
                    if k == 1 and 0 <= i - 2:
                        weight_exp(i - 2)
            weight_exp(B - 1)

            def copy_xT(j, u):
                act.wait_ge(xT_ready, j + 1)
                if not (isinstance(j, int) and j < 2):
                    act.wait_ge(h3_ready, j - 1)
                act.activation(xT[:, u].rearrange("p c s -> p (c s)"), ps_x[:, 0:D], ACT.Copy).then_inc(xT_read, 1)

            def silu(j, u):
                act.wait_ge(h1_ready, j + 1)
                if not (isinstance(j, int) and j < 1):
                    act.wait_ge(g_done, j)
                act.activation(sil, ps_h1[u][:, :], ACT.Silu).then_inc(sil_done, 1)

            def copy_gT(j):
                act.wait_ge(gT_ready, j + 1)
                if not (isinstance(j, int) and j < 1):
                    act.wait_ge(y2_ready, j)
                act.activation(gT.rearrange("p c s -> p (c s)"), ps_g[:, :], ACT.Copy).then_inc(gT_read, 1)

            act.wait_ge(table, TABLE)
            copy_xT(0, 0)
            for j in range(NT):
                silu(j, j % 2)
                if j > 0:
                    copy_gT(j - 1)
                if j + 1 < NT:
                    copy_xT(j + 1, (j + 1) % 2)
            copy_gT(NT - 1)
            act.wait_ge(added[0], 16 * ((NT + 1) // 2))
            act.wait_ge(added[1], 16 * (NT // 2))

        @block.vector
        def _(dve):
            dve.memset(kst[32:64, :, :], 1.0).then_inc(ones_k, 1)
            dve.wait_ge(in_k, 16)
            dve.tensor_copy(kp[:, 0, :], kin).then_inc(k_split, 1)
            dve.wait_ge(k_split, 1)
            dve.tensor_tensor(kres, kin, kp[:, 0, :], ALU.subtract).then_inc(k_split, 1)
            dve.wait_ge(k_split, 2)
            dve.tensor_copy(kp[:, 1, :], kres).then_inc(k_split, 1)
            dve.wait_ge(k_split, 3)
            dve.tensor_tensor(kp[:, 2, :], kres, kp[:, 1, :], ALU.subtract).then_inc(k_split, 1)
            dve.wait_ge(in_const, 48)
            dve.tensor_copy(identb[:, :], ident).then_inc(const_b, 1)
            dve.tensor_copy(trib[:, :], cst[:, C_TRI:C_TRI + P]).then_inc(const_b, 1)
            dve.tensor_copy(onesb[:, :], cst[:, C_ONE:C_ONE + P]).then_inc(const_b, 1)

            def statistics(src, n, b, done):
                dve.bn_stats(stat[:, n, 0:6], src).then_inc(done, 1)
                dve.wait_ge(done, LN * b + 1)
                dve.bn_aggr(mv[:, n, :], stat[:, n, 0:6]).then_inc(done, 1)
                dve.wait_ge(done, LN * b + 2)
                dve.tensor_scalar(rs[:, n, 0:1], mv[:, n, 1:2], EPS, None, ALU.add).then_inc(done, 1)
                dve.wait_ge(done, LN * b + 3)
                dve.tensor_scalar(rs[:, n, 1:2].bitcast(I32), rs[:, n, 0:1].bitcast(I32), -0.5, float(0x5F3759DF),
                                  ALU.mult, ALU.add).then_inc(done, 1)

            def statistics1(b):
                dve.wait_ge(in_x[b % 2], 16 * (b // 2 + 1))
                statistics(xin[:, b % 2, :], 0, b, ln1)

            def apply1(b):
                dve.wait_ge(root1, ROOT * (b + 1))
                if b >= 2:
                    dve.wait_ge(qT_ready, b - 1)
                dve.tensor_scalar(xn1[:, b % 2, :], xin[:, b % 2, :], mv[:, 0, 0:1], rs[:, 0, 1:2],
                                  ALU.subtract, ALU.mult).then_inc(ln1, 1)

            def statistics2(b):
                dve.wait_ge(x2_ready, b + 1)
                statistics(x2[:, b % 2, :], 1, b, ln2)

            def apply2(b):
                dve.wait_ge(root2, ROOT * (b + 1))
                if b >= 2:
                    dve.wait_ge(rows_out[b % 2], 32 * (b // 2))
                    dve.wait_ge(xT2_ready, b - 1)
                dve.tensor_scalar(rows[:, b % 2, 0, 0:D], x2[:, b % 2, :], mv[:, 1, 0:1], rs[:, 1, 1:2],
                                  ALU.subtract, ALU.mult).then_inc(ln2, 1)

            def q_residual1(b):
                dve.wait_ge(q_part, 2 * b + 1)
                dve.tensor_tensor(qres[:, b % 2, :], ps_a[:, 0:D], qp[:, b % 2, 0, :], ALU.subtract)\
                    .then_inc(q_res, 1)

            def q_residual2(b):
                dve.wait_ge(q_part, 2 * b + 2)
                dve.tensor_tensor(qp[:, b % 2, 2, :], qres[:, b % 2, :], qp[:, b % 2, 1, :], ALU.subtract)\
                    .then_inc(q_res, 1)

            def maxima(b, g):
                dve.wait_ge(s_ready, 8 * b + g + 1)
                dve.tensor_reduce(negm[:, b % 2, g * G:(g + 1) * G],
                                  ps_s[g % 2][:, :].rearrange("p (h t) -> p h t", h=G), AX.X, ALU.max,
                                  negate=True).then_inc(max_done, 1)

            def split_neg(b):
                dve.wait_ge(max_done, 8 * b + 8)
                if b >= 2:
                    dve.wait_ge(negT_ready, b - 1)
                m, r, q = negm[:, b % 2, :], negr[:, b % 2, :], negp[:, b % 2]
                dve.tensor_copy(q[:, 0, :], m).then_inc(neg_step, 1)
                dve.wait_ge(neg_step, 4 * b + 1)
                dve.tensor_tensor(r, m, q[:, 0, :], ALU.subtract).then_inc(neg_step, 1)
                dve.wait_ge(neg_step, 4 * b + 2)
                dve.tensor_copy(q[:, 1, :], r).then_inc(neg_step, 1)
                dve.wait_ge(neg_step, 4 * b + 3)
                dve.tensor_tensor(q[:, 2, :], r, q[:, 1, :], ALU.subtract).then_inc(neg_step, 1)

            def normalise(b):
                dve.wait_ge(y_ready, b + 1)
                y = ps_b[:, 0:G * OT].rearrange("p (g k c) -> p g k c", g=G, k=KV)
                r = rden[:, :].rearrange("p (g k) -> p g k", g=G)
                dve.reciprocal(r, y[:, :, :, HD]).then_inc(y_step, 1)
                dve.wait_ge(y_step, 2 * b + 1)
                if b >= 2:
                    dve.wait_ge(x2_ready, b - 1)
                dve.tensor_tensor(att[:, b % 2, :].rearrange("p (k g d) -> p g k d", g=G, d=HD),
                                  y[:, :, :, 0:HD], r[:, :, :, None].broadcast_to((P, G, KV, HD)), ALU.mult)\
                    .then_inc(y_step, 1)

            def choose(b):
                dve.wait_ge(lg_ready, b + 1)
                n = ROUTE * b
                dve.tensor_copy(lg[:, :], ps_b[:, 0:E]).then_inc(route, 1)
                dve.wait_ge(route, n + 1)
                dve.max(top[:, :], lg[:, :]).then_inc(route, 1)
                dve.wait_ge(route, n + 2)
                if b >= 1:
                    dve.wait_ge(w_exp, b)
                dve.tensor_tensor(dlt[:, 0:1], top[:, 1:2], top[:, 0:1], ALU.subtract).then_inc(route, 1)
                dve.max_index(topi[:, :], top[:, :], lg[:, :]).then_inc(route, 1)
                dve.wait_ge(route, n + 4)
                dve.tensor_copy(topf[:, :], topi[:, 0:TOPK]).then_inc(route, 1)
                dve.wait_ge(route, n + 5)
                if b >= 2:
                    dve.wait_ge(seen_ready, b)
                    dve.wait_ge(rank_ready, b - 1)
                hk = hot[:, b % 2]
                dve.tensor_tensor(hk, cst[:, None, C_IOTA:C_IOTA + E].broadcast_to((P, TOPK, E)),
                                  topf[:, :, None].broadcast_to((P, TOPK, E)), ALU.is_equal).then_inc(hot_done, 1)
                dve.wait_ge(hot_done, b + 1)
                dve.tensor_tensor(hotb[:, b % 2, :], hk[:, 0, :], hk[:, 1, :], ALU.add).then_inc(route, 1)

            def weigh(b):
                dve.wait_ge(w_exp, b + 1)
                if b >= 2:
                    dve.wait_ge(rows_out[b % 2], 32 * (b // 2))
                dve.tensor_scalar(dlt[:, 2:3], dlt[:, 1:2], 1.0, None, ALU.add).then_inc(w_step, 1)
                dve.wait_ge(w_step, 3 * b + 1)
                dve.reciprocal(rows[:, b % 2, 0, D + 1:D + 2], dlt[:, 2:3]).then_inc(w_step, 1)
                dve.wait_ge(w_step, 3 * b + 2)
                dve.tensor_tensor(rows[:, b % 2, 1, D + 1:D + 2], dlt[:, 1:2], rows[:, b % 2, 0, D + 1:D + 2],
                                  ALU.mult).then_inc(w_step, 1)

            def place(b):
                dve.wait_ge(rank_ready, b + 1)
                n = POS * b
                dve.tensor_tensor(pos[:, :], ps_a[:, 0:E], cst[:, C_BASE:C_BASE + E], ALU.add).then_inc(pos_step, 1)
                dve.wait_ge(pos_step, n + 1)
                dve.tensor_tensor(posk[:, :, :], hot[:, b % 2], pos[:, None, :].broadcast_to((P, TOPK, E)), ALU.mult)\
                    .then_inc(pos_step, 1)
                dve.wait_ge(pos_step, n + 2)
                if b >= 2:
                    dve.wait_ge(rows_out[b % 2], 32 * (b // 2))
                with nc.allow_low_precision(reason="slot numbers are whole and below 2**24"):
                    dve.tensor_reduce(slot[:, b % 2, :], posk[:, :, :], AX.X, ALU.add).then_inc(pos_step, 1)

            statistics1(0)
            apply1(0)
            for i in range(-2, B + 2):
                if 0 <= i + 1 < B:
                    for g in range(2):
                        maxima(i + 1, g)
                if 0 <= i + 2 < B:
                    q_residual1(i + 2)
                if 0 <= i + 1 < B:
                    for g in range(2, 5):
                        maxima(i + 1, g)
                if 0 <= i - 1 < B:
                    normalise(i - 1)
                if 0 <= i + 1 < B:
                    for g in range(5, 8):
                        maxima(i + 1, g)
                if 0 <= i - 1 < B:
                    statistics2(i - 1)
                if 0 <= i + 3 < B:
                    statistics1(i + 3)
                if 0 <= i + 1 < B:
                    split_neg(i + 1)
                if 0 <= i + 2 < B:
                    q_residual2(i + 2)
                if 0 <= i - 2 < B:
                    if i - 2 < B - 1:
                        weigh(i - 2)
                    place(i - 2)
                if 0 <= i - 1 < B:
                    apply2(i - 1)
                if 0 <= i + 3 < B:
                    apply1(i + 3)
                if 0 <= i - 1 < B:
                    choose(i - 1)
                if i - 1 == B - 1:
                    weigh(B - 1)

            step = [0]

            def link(ins):
                step[0] += 1
                ins.then_inc(table, 1)
                dve.wait_ge(table, step[0])

            dve.wait_ge(cnt_ready, 1)
            bc = (P, NT, E)
            link(dve.tensor_scalar(cnti[:, 0, :], ps_a[:, 0:E], float(P - 1), None, ALU.add))
            link(dve.tensor_scalar(cnti[:, 1, :], cnti[:, 0, :], 7, None, ALU.arith_shift_right))
            link(dve.tensor_copy(ntl[:, :], cnti[:, 1, :]))
            link(dve.tensor_tensor_scan(cum[:, :], cst[:, C_ONE:C_ONE + E], ntl[:, :], 0.0, ALU.mult, ALU.add))
            link(dve.tensor_tensor(dst[:, :], ps_a[:, 0:E], cst[:, C_BASE:C_BASE + E], ALU.add))
            tiles = cst[:, C_TILE:C_TILE + NT]
            link(dve.tensor_tensor(ge[:, :, :], tiles[:, :, None].broadcast_to(bc),
                                   cum[:, None, :].broadcast_to(bc), ALU.is_ge))
            link(dve.tensor_tensor(gn[:, :, :], ge[:, :, :], ntl[:, None, :].broadcast_to(bc), ALU.mult))
            link(dve.tensor_reduce(te[:, :], ge[:, :, :], AX.X, ALU.add))
            link(dve.tensor_reduce(tx[:, :], gn[:, :, :], AX.X, ALU.add))
            link(dve.tensor_tensor(tx[:, :], tiles, tx[:, :], ALU.subtract))
            link(dve.tensor_scalar(ta[:, :], te[:, :], float(REGION), None, ALU.mult))
            link(dve.scalar_tensor_tensor(ta[:, :], tx[:, :], float(P), ta[:, :], ALU.mult, ALU.add))
            link(dve.tensor_scalar(row0[:, :], ta[:, :], float(E * REGION), None, ALU.min))
            link(dve.tensor_scalar(texp[:, :], te[:, :], float(E - 1), None, ALU.min))

            def copy_meta(j, u):
                dve.wait_ge(xs_in[u], 16 * (j // 2 + 1) if isinstance(j, int) else (j - u) * 8 + 16)
                if not (isinstance(j, int) and j < 2):
                    dve.wait_ge(added[u], 16 * (j // 2) if isinstance(j, int) else (j - u) * 8)
                dve.tensor_copy(meta[:, u, :], xs[:, u, D:D + 2]).then_inc(meta_done, 1)

            def gate_h(j, u):
                dve.wait_ge(sil_done, j + 1)
                dve.wait_ge(h3_ready, j + 1)
                if not (isinstance(j, int) and j < 2):
                    dve.wait_ge(gT_ready, j - 1)
                dve.tensor_tensor(gat[:, u, :], ps_h3[u][:, :], sil, ALU.mult).then_inc(g_done, 1)

            def scale_y(j, u):
                dve.wait_ge(y2_ready, j + 1)
                dve.wait_ge(meta_done, j + 1)
                if not (isinstance(j, int) and j < 2):
                    dve.wait_ge(added[u], 16 * (j // 2) if isinstance(j, int) else (j - u) * 8)
                dve.tensor_scalar(ys[:, u, :], ps_y[:, 0:D], meta[:, u, 1:2], None, ALU.mult).then_inc(y2_read, 1)

            for j in range(NT):
                copy_meta(j, j % 2)
                if j > 0:
                    scale_y(j - 1, (j - 1) % 2)
                gate_h(j, j % 2)
            scale_y(NT - 1, (NT - 1) % 2)


def kernel(x, ctx_512, L0_ffn_gate_w, L0_ffn_w1, L0_ffn_w2, L0_ffn_w3):
    import numpy as np
    import concourse.bacc as bacc
    from concourse.bass_utils import run_bass_kernel_spmd

    x, c = np.asarray(x), np.asarray(ctx_512)
    gw, w1, w2, w3 = (np.asarray(a) for a in (L0_ffn_gate_w, L0_ffn_w1, L0_ffn_w2, L0_ffn_w3))

    def up(w):
        return w.reshape(E, F, KC, P).transpose(3, 0, 2, 1).reshape(P, E * KC * F)

    cf, ci = constants()
    arrays = {
        "x": x.reshape(T, D),
        "kT": c.reshape(B, P, KV, HD).transpose(0, 3, 2, 1).reshape(P, KV * P),
        "v": c.reshape(T, KV * HD),
        "gateT": gw.reshape(E, KC, P).transpose(2, 1, 0),
        "w1T": up(w1),
        "w3T": up(w3),
        "w2T": w2.reshape(E, D, FC, P).transpose(3, 0, 2, 1).reshape(P, E * FC * D),
        "cf": cf,
        "ci": ci,
    }
    arrays = {f"in_{n}": np.ascontiguousarray(a) for n, a in arrays.items()}
    nc = bacc.Bacc("TRN2", target_bir_lowering=False, num_devices=1)
    args = [nc.dram_tensor(n, a.shape, mybir.dt.from_np(a.dtype), kind="ExternalInput").ap()
            for n, a in arrays.items()]
    out = nc.dram_tensor("out_rows", (T + P, D), F32, kind="ExternalOutput").ap()
    build(nc, *args, out)
    r = run_bass_kernel_spmd(nc, [arrays], core_ids=[0])
    return r.results[0]["out_rows"][:T].reshape(B, P, D)
```

```python
from contextlib import ExitStack

import concourse.bass as bass
from concourse import mybir
from concourse.bass import IndirectOffsetOnAxis

ALU = mybir.AluOpType
ACT = mybir.ActivationFunctionType
AX = mybir.AxisListType
F32 = mybir.dt.float32
BF16 = mybir.dt.bfloat16
I32 = mybir.dt.int32
U32 = mybir.dt.uint32

P = 128
B, D, KV, G, HD = 16, 256, 8, 4, 8
H = KV * G
T = B * P
E, F, TOPK = 8, 512, 2
KC, FC = D // P, F // P
EPS = 1e-5
SCALE = 1.0 / float(HD) ** 0.5

TERMS = [(0, 0), (0, 1), (0, 2), (1, 0), (1, 1), (2, 0)]
QK_ROWS = len(TERMS) * HD
QKM_ROWS = QK_ROWS + 3
VW = HD + 1
OT = KV * VW

REGION = T + P
RW = D + 2
NT = (TOPK * T + E * (P - 1)) // P

C_ID, C_TRI, C_ONE, C_IOTA, C_BASE, C_TILE, C_END = 0, 128, 256, 384, 392, 400, 400 + NT


def constants():
    import numpy as np
    c = np.zeros((P, C_END), np.float32)
    p = np.arange(P)
    c[:, C_ID:C_ID + P] = np.eye(P)
    c[:, C_TRI:C_TRI + P] = p[:, None] < p[None, :]
    c[:, C_ONE:C_ONE + P] = 1.0
    c[:, C_IOTA:C_IOTA + E] = np.arange(E)
    c[:, C_BASE:C_BASE + E] = np.arange(E) * REGION
    c[:, C_TILE:C_TILE + NT] = np.arange(NT)
    i = (np.arange(B + 1)[None, :] * P + p[:, None]).astype(np.int32)
    return c, i


def build(nc, x, kT, v, gateT, w1T, w3T, w2T, cf, ci, out):
    kparts_d = nc.dram_tensor("kparts_d", (3, P, KV * P), BF16, kind="Internal").ap()
    qparts_d = nc.dram_tensor("qparts_d", (B, 3, D, P), BF16, kind="Internal").ap()
    slots_d = nc.dram_tensor("slots_d", (E * REGION + P, RW), F32, kind="Internal").ap()

    with ExitStack() as ctx:
        def sb(name, shape, dt=F32):
            return ctx.enter_context(nc.sbuf_tensor(name, shape, dt))

        def sem(name):
            return ctx.enter_context(nc.semaphore(name))

        def sems(name, n):
            return [sem(f"{name}{i}") for i in range(n)]

        w13 = sb("w13", [P, 2, E * KC * F])
        w2 = sb("w2", [P, E * FC * D])
        gate = sb("gate", [P, KC, E])
        cst = sb("cst", [P, C_END])
        tok_id = sb("tok_id", [P, B + 1], I32)
        ident = cst[:, C_ID:C_ID + P]
        identb = sb("identb", [P, P], BF16)
        trib = sb("trib", [P, P], BF16)
        onesb = sb("onesb", [P, P], BF16)
        kst = sb("kst", [64, B, KV * P], BF16)
        vnat = sb("vnat", [P, B, KV, HD])
        vblk = sb("vblk", [P, 2, KV * (OT + VW)])
        arena = sb("arena", [P, 3 * H * P // 2])
        qst = arena[:, :].bitcast(BF16).rearrange("p (r h s) -> p r h s", r=3, h=H)
        prob = sb("prob", [P, 4, G * P])
        xin = sb("xin", [P, 2, D])
        xn1 = sb("xn1", [P, 2, D])
        qp = sb("qp", [P, 2, 3, D], BF16)
        qres = sb("qres", [P, 2, D])
        negm = sb("negm", [P, 2, H])
        negp = sb("negp", [P, 2, 3, H], BF16)
        negr = sb("negr", [P, 2, H])
        negT = sb("negT", [3 * H, 2, P], BF16)
        oT = sb("oT", [OT, 2, G * P])
        rden = sb("rden", [P, H])
        att = sb("att", [P, 2, D])
        xres = sb("xres", [P, 2, D])
        x2 = sb("x2", [P, 2, D])
        stat = sb("stat", [P, 2, 8])
        mv = sb("mv", [P, 2, 2])
        rs = sb("rs", [P, 2, 4])
        rows = sb("rows", [P, 2, TOPK, RW])
        xn2T = sb("xn2T", [P, 2, KC, P])
        lg = sb("lg", [P, E])
        top = sb("top", [P, 8])
        topi = sb("topi", [P, 8], U32)
        topf = sb("topf", [P, TOPK])
        hot = sb("hot", [P, 2, TOPK, E])
        hotb = sb("hotb", [P, 2, E], BF16)
        seen = sb("seen", [P, 2, E], BF16)
        dlt = sb("dlt", [P, 4])
        pos = sb("pos", [P, E])
        posk = sb("posk", [P, TOPK, E])
        slot = sb("slot", [P, 2, TOPK], I32)
        kin = arena[:, 0:1024]
        kres = arena[:, 1024:2048]
        kp = arena[:, 2048:2048 + 1536].bitcast(BF16).rearrange("p (j n) -> p j n", j=3)
        cnt = sb("cnt", [P, E])
        cnti = sb("cnti", [P, 2, E], I32)
        ntl = sb("ntl", [P, E])
        cum = sb("cum", [P, E])
        ge = sb("ge", [P, NT, E])
        gn = sb("gn", [P, NT, E])
        te = sb("te", [P, NT])
        tx = sb("tx", [P, NT])
        ta = sb("ta", [P, NT])
        row0 = sb("row0", [P, NT], I32)
        texp = sb("texp", [P, NT], I32)
        dst = sb("dst", [P, E], I32)
        pad = sb("pad", [P, RW])
        at = 0

        def part(n):
            nonlocal at
            at += n
            return arena[:, at - n:at]

        xs = part(2 * RW).rearrange("p (u c) -> p u c", u=2)
        xT = part(2 * D).rearrange("p (u k s) -> p u k s", u=2, k=KC)
        sil = part(F)
        gat = part(2 * F).rearrange("p (u f) -> p u f", u=2)
        gT = part(F).rearrange("p (c s) -> p c s", c=FC)
        ys = part(2 * D).rearrange("p (u c) -> p u c", u=2)
        meta = part(4).rearrange("p (u c) -> p u c", u=2)

        bank = [ctx.enter_context(nc.psum_tensor(f"bank{i}", [P, 512], F32)) for i in range(8)]
        ps_s = bank[0:2]
        ps_e = bank[2:4]
        ps_o = bank[4:6]
        ps_a, ps_b = bank[6], bank[7]
        ps_h1, ps_h3 = bank[0:2], bank[2:4]
        ps_g, ps_y, ps_x = bank[4], bank[5], bank[6]

        in_const, in_k, in_v, in_w = sem("in_const"), sem("in_k"), sem("in_v"), sem("in_w")
        in_x, in_res = sems("in_x", 2), sems("in_res", 2)
        kparts_out, kst_in = sem("kparts_out"), sem("kst_in")
        qparts_out, qst_in = sems("qparts_out", 2), sems("qst_in", 3)
        neg_in = sems("neg_in", 3)
        x2_out, rows_out = sems("x2_out", 2), sems("rows_out", 2)
        pad_row, pads_out = sem("pad_row"), sem("pads_out")
        const_b, k_split = sem("const_b"), sem("k_split")
        v_zero, v_ready = sem("v_zero"), sem("v_ready")
        ln1, ln2, root1, root2 = sem("ln1"), sem("ln2"), sem("root1"), sem("root2")
        qT_ready, q_part, q_res = sem("qT_ready"), sem("q_part"), sem("q_res")
        s_ready, max_done = sem("s_ready"), sem("max_done")
        neg_step, negT_ready, negT_read = sem("neg_step"), sem("negT_ready"), sem("negT_read")
        e_ready, exp_done, pv_done = sem("e_ready"), sem("exp_done"), sem("pv_done")
        oT_read, y_ready, y_step = sem("oT_read"), sem("y_ready"), sem("y_step")
        x2_ready, row_copied, tok_put = sem("x2_ready"), sem("row_copied"), sem("tok_put")
        xT2_ready, xT2_read, lg_ready, route = sem("xT2_ready"), sem("xT2_read"), sem("lg_ready"), sem("route")
        w_exp, w_step, hot_done = sem("w_exp"), sem("w_step"), sem("hot_done")
        seen_ready, rank_ready, pos_step = sem("seen_ready"), sem("rank_ready"), sem("pos_step")
        cnt_ready, table = sem("cnt_ready"), sem("table")
        xs_in = sems("xs_in", 2)
        xT_ready, xT_read, h1_ready, h3_ready = sem("xT_ready"), sem("xT_read"), sem("h1_ready"), sem("h3_ready")
        sil_done, g_done, gT_ready, gT_read = sem("sil_done"), sem("g_done"), sem("gT_ready"), sem("gT_read")
        y2_ready, y2_read, meta_done, added = sem("y2_ready"), sem("y2_read"), sem("meta_done"), sems("added", 2)

        LN, ROOT, ROUTE, POS, TABLE = 5, 8, 6, 3, 14
        W_PIECES = 8

        block = ctx.enter_context(nc.Block())

        @block.sync
        def _(sp):
            for b in range(2):
                sp.dma_start(xin[:, b, :], x[b * P:(b + 1) * P, :]).then_inc(in_x[b], 16)
            sp.dma_start(tok_id[:, :], ci).then_inc(in_const, 16)
            sp.dma_start(gate[:, :, :], gateT).then_inc(in_const, 16)
            sp.dma_start(vnat[:, :, :, :], v.rearrange("(b t) (k d) -> t b k d", t=P, k=KV)).then_inc(in_v, 16)
            sp.wait_ge(const_b, 1)
            for j in range(3):
                sp.dma_start(kst[QK_ROWS + j:QK_ROWS + j + 1, :, :], onesb[:, :]).then_inc(kst_in, 16)
            sp.wait_ge(k_split, 4)
            sp.dma_start(kparts_d.rearrange("j p n -> p j n"), kp).then_inc(kparts_out, 16)
            sp.wait_ge(kparts_out, 16)
            kd = kparts_d.rearrange("j (b d) n -> j d b n", d=HD)
            for i, (_, j) in enumerate(TERMS):
                sp.dma_start(kst[i * HD:(i + 1) * HD, :, :], kd[j]).then_inc(kst_in, 16)

            def load_x(b):
                sp.wait_ge(ln1, LN * (b - 1))
                sp.dma_start(xin[:, b % 2, :], x[b * P:(b + 1) * P, :]).then_inc(in_x[b % 2], 16)

            def load_res(b):
                if b >= 2:
                    sp.wait_ge(x2_ready, b - 1)
                sp.dma_start(xres[:, b % 2, :], x[b * P:(b + 1) * P, :]).then_inc(in_res[b % 2], 16)

            def store_x2(b):
                sp.wait_ge(x2_ready, b + 1)
                sp.dma_start(out[b * P:(b + 1) * P, :], x2[:, b % 2, :]).then_inc(x2_out[b % 2], 16)

            def write_q(b):
                sp.wait_ge(q_res, 2 * b + 2)
                sp.dma_start(qparts_d[b].rearrange("j (c p) s -> p j c s", c=KC),
                             qp[:, b % 2].rearrange("p j (c s) -> p j c s", c=KC))\
                    .then_inc(qparts_out[b % 2], 16)

            def stack_q(b):
                sp.wait_ge(qparts_out[b % 2], 16 * (b // 2 + 1))
                if b >= 3:
                    sp.wait_ge(e_ready, 8 * (b - 2))
                if b == 0:
                    sp.wait_ge(kparts_out, 16)
                qd = qparts_d[b].rearrange("j (h d) s -> j d h s", d=HD)
                for i, (j, _) in enumerate(TERMS):
                    sp.dma_start(qst[i * HD:(i + 1) * HD, b % 3, :, :], qd[j]).then_inc(qst_in[b % 3], 16)

            def lay_neg(b):
                sp.wait_ge(negT_read, b + 1)
                if b >= 3:
                    sp.wait_ge(e_ready, 8 * (b - 2))
                sp.dma_start(qst[QK_ROWS:QKM_ROWS, b % 3, :, :],
                             negT[:, b % 2, :]).then_inc(neg_in[b % 3], 16)

            def load_weights(n):
                m, piece = n // W_PIECES, E * KC * F // W_PIECES
                c = slice((n % W_PIECES) * piece, (n % W_PIECES + 1) * piece)
                to, frm = [(w13[:, 0, c], w1T[:, c]), (w13[:, 1, c], w3T[:, c]), (w2[:, c], w2T[:, c])][m]
                sp.dma_start(to, frm).then_inc(in_w, 16)

            for i in range(-3, B + 1):
                if 0 <= i + 2 < B:
                    stack_q(i + 2)
                if 2 <= i + 5 < B:
                    load_x(i + 5)
                if 0 <= i < B:
                    load_res(i)
                    load_weights(i)
                if 0 <= i + 1 < B:
                    lay_neg(i + 1)
                if 0 <= i + 3 < B:
                    write_q(i + 3)
                if 0 <= i - 1 < B:
                    store_x2(i - 1)
                if 0 <= i < 3 * W_PIECES - B:
                    load_weights(B + i)

            sp.wait_ge(pad_row, 3)
            sp.dma_start(out[T:T + P, :], pad[:, 0:D]).then_inc(pads_out, 16)
            sp.dma_start(slots_d[E * REGION:E * REGION + P, :], pad[:, :]).then_inc(pads_out, 16)
            sp.wait_ge(table, TABLE)
            for e in range(E):
                r = sp.value_load(dst[0:1, e:e + 1], min_val=e * REGION, max_val=e * REGION + T)
                sp.dma_start(slots_d[bass.ds(r, P), :], pad[:, :]).then_inc(pads_out, 16)
            sp.wait_ge(pads_out, 16 * (E + 2))
            for u in range(2):
                sp.wait_ge(rows_out[u], 16 * B)
                sp.wait_ge(x2_out[u], 16 * B // 2)

            def load_tile(j, u):
                r = sp.value_load(row0[0:1, bass.ds(j, 1)], min_val=0, max_val=E * REGION)
                if not (isinstance(j, int) and j < 2):
                    sp.wait_ge(xT_ready, j - 1)
                    sp.wait_ge(meta_done, j - 1)
                sp.dma_start(xs[:, u, :], slots_d[bass.ds(r, P), :]).then_inc(xs_in[u], 16)

            for j in range(NT):
                load_tile(j, j % 2)

        @block.gpsimd
        def _(pool):
            pool.memset(vblk[:, :, :], 0.0).then_inc(v_zero, 1)
            pool.memset(seen[:, 0, :], 0.0).then_inc(seen_ready, 1)
            pool.wait_ge(v_zero, 1)
            vb = vblk[:, :, :].rearrange("p u (k r) -> p u k r", k=KV)
            for u in range(2):
                pool.memset(vb[:, u, :, HD:HD + 1], 1.0).then_inc(v_zero, 1)
            pool.memset(pad[:, :], 0.0).then_inc(pad_row, 1)
            pool.wait_ge(pad_row, 1)
            pool.wait_ge(in_const, 48)
            pool.tensor_copy(pad[:, D:D + 1].bitcast(I32), tok_id[:, B:B + 1]).then_inc(pad_row, 2)
            pool.wait_ge(in_v, 16)
            pool.wait_ge(v_zero, 3)

            def put_v(b):
                if b >= 2:
                    pool.wait_ge(pv_done, 8 * (b - 1))
                pool.tensor_copy(vb[:, b % 2, :, 0:HD], vnat[:, b]).then_inc(v_ready, 1)

            def add_res(b):
                pool.wait_ge(y_step, 2 * b + 2)
                pool.wait_ge(in_res[b % 2], 16 * (b // 2 + 1))
                if b >= 2:
                    pool.wait_ge(x2_out[b % 2], 16 * (b // 2))
                    pool.wait_ge(ln2, LN * (b - 1))
                pool.tensor_tensor(x2[:, b % 2, :], att[:, b % 2, :], xres[:, b % 2, :], ALU.add)\
                    .then_inc(x2_ready, 1)

            def put_token(b):
                if b >= 2:
                    pool.wait_ge(rows_out[b % 2], 32 * (b // 2))
                for k in range(TOPK):
                    pool.tensor_copy(rows[:, b % 2, k, D:D + 1].bitcast(I32), tok_id[:, b:b + 1])\
                        .then_inc(tok_put, 1)

            def add_seen(b):
                pool.wait_ge(route, ROUTE * b + 6)
                pool.wait_ge(seen_ready, b + 1)
                if b >= 1:
                    pool.wait_ge(rank_ready, b)
                pool.tensor_tensor(seen[:, (b + 1) % 2, :], seen[:, b % 2, :], hotb[:, b % 2, :], ALU.add)\
                    .then_inc(seen_ready, 1)

            def scatter(b):
                pool.wait_ge(pos_step, POS * b + 3)
                pool.wait_ge(row_copied, b + 1)
                pool.wait_ge(w_step, 3 * b + 3)
                pool.wait_ge(tok_put, 2 * b + 2)
                for k in range(TOPK):
                    pool.indirect_dma_start(
                        slots_d, IndirectOffsetOnAxis(ap=slot[:, b % 2, k:k + 1], axis=0),
                        rows[:, b % 2, k, :], None).then_inc(rows_out[b % 2], 16)

            def root(n, b, guessed, done):
                v, y, h, p = (rs[:, n, c:c + 1] for c in range(4))
                pool.wait_ge(guessed, LN * b + 4)
                for r in range(0, ROOT, 4):
                    pool.tensor_scalar(h, y, y, v, ALU.mult, ALU.mult).then_inc(done, 1)
                    pool.wait_ge(done, ROOT * b + r + 1)
                    pool.tensor_scalar(p, h, 3 / 8, -10 / 8, ALU.mult, ALU.add).then_inc(done, 1)
                    pool.wait_ge(done, ROOT * b + r + 2)
                    pool.tensor_scalar(p, p, h, 15 / 8, ALU.mult, ALU.add).then_inc(done, 1)
                    pool.wait_ge(done, ROOT * b + r + 3)
                    pool.tensor_tensor(y, y, p, ALU.mult).then_inc(done, 1)
                    if r + 4 < ROOT:
                        pool.wait_ge(done, ROOT * b + r + 4)

            root(0, 0, ln1, root1)
            for i in range(-3, B + 3):
                if 0 <= i + 1 < B:
                    put_v(i + 1)
                if 0 <= i - 3 < B:
                    scatter(i - 3)
                if 0 <= i + 4 < B:
                    root(0, i + 4, ln1, root1)
                if 0 <= i - 2 < B:
                    add_seen(i - 2)
                if 0 <= i - 1 < B:
                    add_res(i - 1)
                    root(1, i - 1, ln2, root2)
                    put_token(i - 1)

            pool.wait_ge(pads_out, 16 * (E + 2))
            for u in range(2):
                pool.wait_ge(x2_out[u], 16 * B // 2)

            def add_out(j, u):
                pool.wait_ge(y2_read, j + 1)
                pool.wait_ge(meta_done, j + 1)
                pool.indirect_dma_start(
                    out, IndirectOffsetOnAxis(ap=meta[:, u, 0:1].bitcast(I32), axis=0),
                    ys[:, u, :], None, compute_op=ALU.add).then_inc(added[u], 16)
                pool.wait_ge(added[u], 16 * (j // 2 + 1))

            for j in range(NT):
                add_out(j, j % 2)

        @block.tensor
        def _(pe):
            pe.wait_ge(in_const, 48)
            pe.wait_ge(const_b, 3)

            def q_transpose(b):
                pe.wait_ge(ln1, LN * b + LN)
                if b >= 6:
                    pe.wait_ge(pos_step, POS * (b - 6) + 1)
                elif b >= 3:
                    pe.wait_ge(negT_read, b - 2)
                elif b >= 1:
                    pe.wait_ge(q_res, 2 * b - 1)
                for c in range(KC):
                    m = pe.transpose(ps_a[:, c * P:(c + 1) * P], xn1[:, b % 2, c * P:(c + 1) * P], ident)
                m.then_inc(qT_ready, 1)

            def score_group(b, g):
                if g == 0:
                    pe.wait_ge(qst_in[b % 3], 16 * len(TERMS) * (b // 3 + 1))
                    if b == 0:
                        pe.wait_ge(kst_in, 16 * (len(TERMS) + 3))
                if 8 * b + g >= 2:
                    pe.wait_ge(max_done, 8 * b + g - 1)
                for h in range(G * g, G * g + G):
                    m = pe.matmul(ps_s[g % 2][:, (h % G) * P:(h % G + 1) * P], qst[0:QK_ROWS, b % 3, h, :],
                                  kst[0:QK_ROWS, b, g * P:(g + 1) * P], start=True, stop=True)
                m.then_inc(s_ready, 1)

            def neg_transpose(b):
                pe.wait_ge(neg_step, 4 * b + 4)
                if b + 2 < B:
                    pe.wait_ge(q_res, 2 * (b + 2) + 1)
                else:
                    pe.wait_ge(pos_step, POS * (b - 4) + 1)
                pe.transpose(ps_a[0:3 * H, 0:P // 2].bitcast(BF16), negp[:, b % 2].rearrange("p j h -> p (j h)"),
                             identb[:, :]).then_inc(negT_ready, 1)

            def e_products(b, k):
                if k == 0:
                    pe.wait_ge(neg_in[b % 3], 16 * (b // 3 + 1))
                if 8 * b + k >= 2:
                    pe.wait_ge(exp_done, 8 * b + k - 1)
                pe.matmul(ps_e[k % 2][:, :], kst[0:QKM_ROWS, b, k * P:(k + 1) * P],
                          qst[0:QKM_ROWS, b % 3, k * G:(k + 1) * G, :].rearrange("p h s -> p (h s)"),
                          start=True, stop=True).then_inc(e_ready, 1)

            def pv(b, k):
                if k == 0:
                    pe.wait_ge(v_ready, b + 1)
                    if b >= 2:
                        pe.wait_ge(oT_read, b - 1)
                pe.wait_ge(exp_done, 8 * b + k + 1)
                pe.matmul(ps_o[b % 2][0:OT, :], vblk[:, b % 2, k * OT:(k + 1) * OT], prob[:, k % 4, :],
                          start=(k == 0), stop=(k == KV - 1)).then_inc(pv_done, 1)

            def y_transpose(b):
                pe.wait_ge(oT_read, b + 1)
                if b >= 1:
                    pe.wait_ge(route, ROUTE * (b - 1) + 1)
                for g in range(G):
                    m = pe.transpose(ps_b[:, g * OT:(g + 1) * OT], oT[:, b % 2, g * P:(g + 1) * P],
                                     ident[0:OT, 0:OT])
                m.then_inc(y_ready, 1)

            def x2_transpose(b):
                pe.wait_ge(ln2, LN * b + LN)
                pe.wait_ge(y_step, 2 * b + 2)
                for c in range(KC):
                    m = pe.transpose(ps_b[:, c * P:(c + 1) * P], rows[:, b % 2, 0, c * P:(c + 1) * P], ident)
                m.then_inc(xT2_ready, 1)

            def logits(b):
                pe.wait_ge(xT2_read, b + 1)
                for c in range(KC):
                    m = pe.matmul(ps_b[:, 0:E], xn2T[:, b % 2, c, :], gate[:, c, :],
                                  start=(c == 0), stop=(c == KC - 1))
                m.then_inc(lg_ready, 1)

            def ranks(b):
                pe.wait_ge(route, ROUTE * b + 6)
                pe.wait_ge(seen_ready, b + 1)
                if b + 3 < B:
                    pe.wait_ge(negT_read, b + 4)
                else:
                    pe.wait_ge(pos_step, POS * (b - 1) + 1)
                pe.matmul(ps_a[:, 0:E], trib[:, :], hotb[:, b % 2, :], start=True, stop=False)
                pe.matmul(ps_a[:, 0:E], onesb[:, :], seen[:, b % 2, :], start=False, stop=True)\
                    .then_inc(rank_ready, 1)

            for i in range(-3, B + 2):
                for k in range(KV):
                    if 0 <= i < B:
                        e_products(i, k)
                    if k == 0 and 0 <= i - 1 < B:
                        pv(i - 1, KV - 1)
                    if k == 1 and 0 <= i + 3 < B:
                        q_transpose(i + 3)
                    if k == 1 and 0 <= i - 2 < B:
                        x2_transpose(i - 2)
                    if k == 2 and 0 <= i - 2 < B:
                        logits(i - 2)
                    if k == 3 and 0 <= i - 1 < B:
                        y_transpose(i - 1)
                    if k < 4 and 0 <= i + 1 < B:
                        score_group(i + 1, k + 4)
                    if k >= 4 and 0 <= i + 2 < B:
                        score_group(i + 2, k - 4)
                    if k == 5 and 0 <= i + 1 < B:
                        neg_transpose(i + 1)
                    if k == 6 and 0 <= i - 2 < B:
                        ranks(i - 2)
                    if k >= 1 and 0 <= i < B:
                        pv(i, k - 1)
            pe.wait_ge(seen_ready, B + 1)
            pe.wait_ge(pos_step, POS * B - 2)
            pe.matmul(ps_a[:, 0:E], onesb[:, :], seen[:, B % 2, :], start=True, stop=True).then_inc(cnt_ready, 1)

            pe.wait_ge(table, TABLE)
            pe.wait_ge(in_w, 16 * 3 * W_PIECES)

            def tile_transpose(j, u):
                pe.wait_ge(xs_in[u], 16 * (j // 2 + 1) if isinstance(j, int) else (j - u) * 8 + 16)
                if not (isinstance(j, int) and j < 1):
                    pe.wait_ge(xT_read, j)
                for c in range(KC):
                    m = pe.transpose(ps_x[:, c * P:(c + 1) * P], xs[:, u, c * P:(c + 1) * P], ident)
                m.then_inc(xT_ready, 1)

            def tile_h(j, u, w, e, bank_, done, used):
                pe.wait_ge(xT_read, j + 1)
                if not (isinstance(j, int) and j < 2):
                    pe.wait_ge(used, j - 1)
                for c in range(KC):
                    m = pe.matmul(bank_[u][:, :], xT[:, u, c, :],
                                  w13[:, w, bass.ds(e * (KC * F) + c * F, F)], start=(c == 0), stop=(c == KC - 1))
                m.then_inc(done, 1)

            def g_transpose(j, u):
                pe.wait_ge(g_done, j + 1)
                if not (isinstance(j, int) and j < 1):
                    pe.wait_ge(gT_read, j)
                for c in range(FC):
                    m = pe.transpose(ps_g[:, c * P:(c + 1) * P], gat[:, u, c * P:(c + 1) * P], ident)
                m.then_inc(gT_ready, 1)

            def tile_y(j, u, e):
                pe.wait_ge(gT_read, j + 1)
                if not (isinstance(j, int) and j < 1):
                    pe.wait_ge(y2_read, j)
                for c in range(FC):
                    m = pe.matmul(ps_y[:, 0:D], gT[:, c, :], w2[:, bass.ds(e * (FC * D) + c * D, D)],
                                  start=(c == 0), stop=(c == FC - 1))
                m.then_inc(y2_ready, 1)

            def expert(j):
                return pe.value_load(texp[0:1, bass.ds(j, 1)], min_val=0, max_val=E - 1)

            tile_transpose(0, 0)
            last = None
            for j in range(NT):
                e = expert(j)
                tile_h(j, j % 2, 0, e, ps_h1, h1_ready, sil_done)
                if j > 0:
                    g_transpose(j - 1, (j - 1) % 2)
                tile_h(j, j % 2, 1, e, ps_h3, h3_ready, g_done)
                if j + 1 < NT:
                    tile_transpose(j + 1, (j + 1) % 2)
                if j > 0:
                    tile_y(j - 1, (j - 1) % 2, last)
                last = e
            g_transpose(NT - 1, (NT - 1) % 2)
            tile_y(NT - 1, (NT - 1) % 2, last)

        @block.scalar
        def _(act):
            act.dma_start(kin, kT).then_inc(in_k, 16)
            act.dma_start(cst[:, :], cf).then_inc(in_const, 16)
            act.wait_ge(in_k, 16)
            act.activation(kp[:, 0, :], kin, ACT.Copy).then_inc(k_split, 1)
            act.wait_ge(k_split, 2)
            act.activation(kp[:, 1, :], kres, ACT.Copy).then_inc(k_split, 1)

            def exps(b, k):
                n = 8 * b + k
                act.wait_ge(e_ready, n + 1)
                if n >= 4:
                    act.wait_ge(pv_done, n - 3)
                act.activation(prob[:, k % 4, :], ps_e[k % 2][:, :], ACT.Exp, scale=SCALE).then_inc(exp_done, 1)

            def q_part1(b):
                act.wait_ge(qT_ready, b + 1)
                if b >= 2:
                    act.wait_ge(qparts_out[b % 2], 16 * (b // 2))
                act.activation(qp[:, b % 2, 0, :], ps_a[:, 0:D], ACT.Copy).then_inc(q_part, 1)

            def q_part2(b):
                act.wait_ge(q_res, 2 * b + 1)
                act.activation(qp[:, b % 2, 1, :], qres[:, b % 2, :], ACT.Copy).then_inc(q_part, 1)

            def copy_oT(b):
                act.wait_ge(pv_done, 8 * b + 8)
                if b >= 2:
                    act.wait_ge(y_ready, b - 1)
                act.activation(oT[:, b % 2, :], ps_o[b % 2][0:OT, :], ACT.Copy).then_inc(oT_read, 1)

            def copy_x2T(b):
                act.wait_ge(xT2_ready, b + 1)
                if b >= 2:
                    act.wait_ge(lg_ready, b - 1)
                act.activation(xn2T[:, b % 2].rearrange("p c s -> p (c s)"), ps_b[:, 0:D], ACT.Copy)\
                    .then_inc(xT2_read, 1)

            def copy_negT(b):
                act.wait_ge(negT_ready, b + 1)
                if b >= 2:
                    act.wait_ge(neg_in[(b - 2) % 3], 16 * ((b - 2) // 3 + 1))
                act.activation(negT[:, b % 2, :], ps_a[0:3 * H, 0:P // 2].bitcast(BF16), ACT.Copy)\
                    .then_inc(negT_read, 1)

            def copy_row(b):
                act.wait_ge(ln2, LN * b + LN)
                act.activation(rows[:, b % 2, 1, 0:D], rows[:, b % 2, 0, 0:D], ACT.Copy).then_inc(row_copied, 1)

            def weight_exp(b):
                act.wait_ge(route, ROUTE * b + 3)
                if b >= 1:
                    act.wait_ge(w_step, 3 * b)
                act.activation(dlt[:, 1:2], dlt[:, 0:1], ACT.Exp).then_inc(w_exp, 1)

            for i in range(-3, B + 2):
                for k in range(KV):
                    if 0 <= i < B:
                        exps(i, k)
                    if k == 0 and 0 <= i - 1 < B:
                        copy_oT(i - 1)
                    if k == 1 and 0 <= i + 3 < B:
                        q_part1(i + 3)
                    if k == 1 and 0 <= i - 2 < B:
                        copy_x2T(i - 2)
                    if k == 2 and 0 <= i - 2 < B:
                        copy_row(i - 2)
                    if k == 3 and 0 <= i + 3 < B:
                        q_part2(i + 3)
                    if k == 5 and 0 <= i + 1 < B:
                        copy_negT(i + 1)
                    if k == 6 and 0 <= i - 2 < B:
                        weight_exp(i - 2)

            def copy_xT(j, u):
                act.wait_ge(xT_ready, j + 1)
                if not (isinstance(j, int) and j < 2):
                    act.wait_ge(h3_ready, j - 1)
                act.activation(xT[:, u].rearrange("p c s -> p (c s)"), ps_x[:, 0:D], ACT.Copy).then_inc(xT_read, 1)

            def silu(j, u):
                act.wait_ge(h1_ready, j + 1)
                if not (isinstance(j, int) and j < 1):
                    act.wait_ge(g_done, j)
                act.activation(sil, ps_h1[u][:, :], ACT.Silu).then_inc(sil_done, 1)

            def copy_gT(j):
                act.wait_ge(gT_ready, j + 1)
                if not (isinstance(j, int) and j < 1):
                    act.wait_ge(y2_ready, j)
                act.activation(gT.rearrange("p c s -> p (c s)"), ps_g[:, :], ACT.Copy).then_inc(gT_read, 1)

            act.wait_ge(table, TABLE)
            copy_xT(0, 0)
            for j in range(NT):
                silu(j, j % 2)
                if j > 0:
                    copy_gT(j - 1)
                if j + 1 < NT:
                    copy_xT(j + 1, (j + 1) % 2)
            copy_gT(NT - 1)
            act.wait_ge(added[0], 16 * ((NT + 1) // 2))
            act.wait_ge(added[1], 16 * (NT // 2))

        @block.vector
        def _(dve):
            def statistics(src, n, b, done):
                dve.bn_stats(stat[:, n, 0:6], src).then_inc(done, 1)
                dve.wait_ge(done, LN * b + 1)
                dve.bn_aggr(mv[:, n, :], stat[:, n, 0:6]).then_inc(done, 1)
                dve.wait_ge(done, LN * b + 2)
                dve.tensor_scalar(rs[:, n, 0:1], mv[:, n, 1:2], EPS, None, ALU.add).then_inc(done, 1)
                dve.wait_ge(done, LN * b + 3)
                dve.tensor_scalar(rs[:, n, 1:2].bitcast(I32), rs[:, n, 0:1].bitcast(I32), -0.5, float(0x5F3759DF),
                                  ALU.mult, ALU.add).then_inc(done, 1)

            def statistics1(b):
                dve.wait_ge(in_x[b % 2], 16 * (b // 2 + 1))
                statistics(xin[:, b % 2, :], 0, b, ln1)

            def apply1(b):
                dve.wait_ge(root1, ROOT * (b + 1))
                if b >= 2:
                    dve.wait_ge(qT_ready, b - 1)
                dve.tensor_scalar(xn1[:, b % 2, :], xin[:, b % 2, :], mv[:, 0, 0:1], rs[:, 0, 1:2],
                                  ALU.subtract, ALU.mult).then_inc(ln1, 1)

            def statistics2(b):
                dve.wait_ge(x2_ready, b + 1)
                statistics(x2[:, b % 2, :], 1, b, ln2)

            def apply2(b):
                dve.wait_ge(root2, ROOT * (b + 1))
                if b >= 2:
                    dve.wait_ge(rows_out[b % 2], 32 * (b // 2))
                    dve.wait_ge(xT2_ready, b - 1)
                dve.tensor_scalar(rows[:, b % 2, 0, 0:D], x2[:, b % 2, :], mv[:, 1, 0:1], rs[:, 1, 1:2],
                                  ALU.subtract, ALU.mult).then_inc(ln2, 1)

            def q_residual1(b):
                dve.wait_ge(q_part, 2 * b + 1)
                dve.tensor_tensor(qres[:, b % 2, :], ps_a[:, 0:D], qp[:, b % 2, 0, :], ALU.subtract)\
                    .then_inc(q_res, 1)

            def q_residual2(b):
                dve.wait_ge(q_part, 2 * b + 2)
                dve.tensor_tensor(qp[:, b % 2, 2, :], qres[:, b % 2, :], qp[:, b % 2, 1, :], ALU.subtract)\
                    .then_inc(q_res, 1)

            def maxima(b, g):
                dve.wait_ge(s_ready, 8 * b + g + 1)
                dve.tensor_reduce(negm[:, b % 2, g * G:(g + 1) * G],
                                  ps_s[g % 2][:, :].rearrange("p (h t) -> p h t", h=G), AX.X, ALU.max,
                                  negate=True).then_inc(max_done, 1)

            def split_neg(b):
                dve.wait_ge(max_done, 8 * b + 8)
                if b >= 2:
                    dve.wait_ge(negT_ready, b - 1)
                m, r, q = negm[:, b % 2, :], negr[:, b % 2, :], negp[:, b % 2]
                dve.tensor_copy(q[:, 0, :], m).then_inc(neg_step, 1)
                dve.wait_ge(neg_step, 4 * b + 1)
                dve.tensor_tensor(r, m, q[:, 0, :], ALU.subtract).then_inc(neg_step, 1)
                dve.wait_ge(neg_step, 4 * b + 2)
                dve.tensor_copy(q[:, 1, :], r).then_inc(neg_step, 1)
                dve.wait_ge(neg_step, 4 * b + 3)
                dve.tensor_tensor(q[:, 2, :], r, q[:, 1, :], ALU.subtract).then_inc(neg_step, 1)

            def normalise(b):
                dve.wait_ge(y_ready, b + 1)
                y = ps_b[:, 0:G * OT].rearrange("p (g k c) -> p g k c", g=G, k=KV)
                r = rden[:, :].rearrange("p (g k) -> p g k", g=G)
                dve.reciprocal(r, y[:, :, :, HD]).then_inc(y_step, 1)
                dve.wait_ge(y_step, 2 * b + 1)
                if b >= 2:
                    dve.wait_ge(x2_ready, b - 1)
                dve.tensor_tensor(att[:, b % 2, :].rearrange("p (k g d) -> p g k d", g=G, d=HD),
                                  y[:, :, :, 0:HD], r[:, :, :, None].broadcast_to((P, G, KV, HD)), ALU.mult)\
                    .then_inc(y_step, 1)

            def choose(b):
                dve.wait_ge(lg_ready, b + 1)
                n = ROUTE * b
                dve.tensor_copy(lg[:, :], ps_b[:, 0:E]).then_inc(route, 1)
                dve.wait_ge(route, n + 1)
                dve.max(top[:, :], lg[:, :]).then_inc(route, 1)
                dve.wait_ge(route, n + 2)
                if b >= 1:
                    dve.wait_ge(w_exp, b)
                dve.tensor_tensor(dlt[:, 0:1], top[:, 1:2], top[:, 0:1], ALU.subtract).then_inc(route, 1)
                dve.max_index(topi[:, :], top[:, :], lg[:, :]).then_inc(route, 1)
                dve.wait_ge(route, n + 4)
                dve.tensor_copy(topf[:, :], topi[:, 0:TOPK]).then_inc(route, 1)
                dve.wait_ge(route, n + 5)
                if b >= 2:
                    dve.wait_ge(seen_ready, b)
                    dve.wait_ge(rank_ready, b - 1)
                hk = hot[:, b % 2]
                dve.tensor_tensor(hk, cst[:, None, C_IOTA:C_IOTA + E].broadcast_to((P, TOPK, E)),
                                  topf[:, :, None].broadcast_to((P, TOPK, E)), ALU.is_equal).then_inc(hot_done, 1)
                dve.wait_ge(hot_done, b + 1)
                dve.tensor_tensor(hotb[:, b % 2, :], hk[:, 0, :], hk[:, 1, :], ALU.add).then_inc(route, 1)

            def weigh(b):
                dve.wait_ge(w_exp, b + 1)
                if b >= 2:
                    dve.wait_ge(rows_out[b % 2], 32 * (b // 2))
                dve.tensor_scalar(dlt[:, 2:3], dlt[:, 1:2], 1.0, None, ALU.add).then_inc(w_step, 1)
                dve.wait_ge(w_step, 3 * b + 1)
                dve.reciprocal(rows[:, b % 2, 0, D + 1:D + 2], dlt[:, 2:3]).then_inc(w_step, 1)
                dve.wait_ge(w_step, 3 * b + 2)
                dve.tensor_tensor(rows[:, b % 2, 1, D + 1:D + 2], dlt[:, 1:2], rows[:, b % 2, 0, D + 1:D + 2],
                                  ALU.mult).then_inc(w_step, 1)

            def place(b):
                dve.wait_ge(rank_ready, b + 1)
                n = POS * b
                dve.tensor_tensor(pos[:, :], ps_a[:, 0:E], cst[:, C_BASE:C_BASE + E], ALU.add).then_inc(pos_step, 1)
                dve.wait_ge(pos_step, n + 1)
                dve.tensor_tensor(posk[:, :, :], hot[:, b % 2], pos[:, None, :].broadcast_to((P, TOPK, E)), ALU.mult)\
                    .then_inc(pos_step, 1)
                dve.wait_ge(pos_step, n + 2)
                if b >= 2:
                    dve.wait_ge(rows_out[b % 2], 32 * (b // 2))
                with nc.allow_low_precision(reason="slot numbers are whole and below 2**24"):
                    dve.tensor_reduce(slot[:, b % 2, :], posk[:, :, :], AX.X, ALU.add).then_inc(pos_step, 1)

            dve.memset(onesb[:, :], 1.0).then_inc(const_b, 1)
            statistics1(0)
            dve.wait_ge(k_split, 1)
            dve.tensor_tensor(kres, kin, kp[:, 0, :], ALU.subtract).then_inc(k_split, 1)
            apply1(0)
            dve.wait_ge(k_split, 3)
            dve.tensor_tensor(kp[:, 2, :], kres, kp[:, 1, :], ALU.subtract).then_inc(k_split, 1)
            dve.wait_ge(in_const, 48)
            dve.tensor_copy(identb[:, :], ident).then_inc(const_b, 1)
            dve.tensor_copy(trib[:, :], cst[:, C_TRI:C_TRI + P]).then_inc(const_b, 1)
            for i in range(-3, B + 3):
                if 0 <= i + 1 < B:
                    maxima(i + 1, 4)
                if 0 <= i + 4 < B:
                    statistics1(i + 4)
                if 0 <= i + 1 < B:
                    maxima(i + 1, 5)
                if 0 <= i + 3 < B:
                    q_residual1(i + 3)
                if 0 <= i + 1 < B:
                    maxima(i + 1, 6)
                if 0 <= i - 2 < B:
                    choose(i - 2)
                if 0 <= i + 1 < B:
                    maxima(i + 1, 7)
                    split_neg(i + 1)
                if 0 <= i - 1 < B:
                    normalise(i - 1)
                if 0 <= i + 2 < B:
                    maxima(i + 2, 0)
                if 0 <= i + 3 < B:
                    q_residual2(i + 3)
                if 0 <= i - 1 < B:
                    statistics2(i - 1)
                if 0 <= i + 2 < B:
                    maxima(i + 2, 1)
                if 0 <= i + 4 < B:
                    apply1(i + 4)
                if 0 <= i + 2 < B:
                    maxima(i + 2, 2)
                if 0 <= i - 2 < B:
                    weigh(i - 2)
                if 0 <= i + 2 < B:
                    maxima(i + 2, 3)
                if 0 <= i - 2 < B:
                    place(i - 2)
                if 0 <= i - 1 < B:
                    apply2(i - 1)

            step = [0]

            def link(ins):
                step[0] += 1
                ins.then_inc(table, 1)
                dve.wait_ge(table, step[0])

            dve.wait_ge(cnt_ready, 1)
            bc = (P, NT, E)
            link(dve.tensor_scalar(cnti[:, 0, :], ps_a[:, 0:E], float(P - 1), None, ALU.add))
            link(dve.tensor_scalar(cnti[:, 1, :], cnti[:, 0, :], 7, None, ALU.arith_shift_right))
            link(dve.tensor_copy(ntl[:, :], cnti[:, 1, :]))
            link(dve.tensor_tensor_scan(cum[:, :], cst[:, C_ONE:C_ONE + E], ntl[:, :], 0.0, ALU.mult, ALU.add))
            link(dve.tensor_tensor(dst[:, :], ps_a[:, 0:E], cst[:, C_BASE:C_BASE + E], ALU.add))
            tiles = cst[:, C_TILE:C_TILE + NT]
            link(dve.tensor_tensor(ge[:, :, :], tiles[:, :, None].broadcast_to(bc),
                                   cum[:, None, :].broadcast_to(bc), ALU.is_ge))
            link(dve.tensor_tensor(gn[:, :, :], ge[:, :, :], ntl[:, None, :].broadcast_to(bc), ALU.mult))
            link(dve.tensor_reduce(te[:, :], ge[:, :, :], AX.X, ALU.add))
            link(dve.tensor_reduce(tx[:, :], gn[:, :, :], AX.X, ALU.add))
            link(dve.tensor_tensor(tx[:, :], tiles, tx[:, :], ALU.subtract))
            link(dve.tensor_scalar(ta[:, :], te[:, :], float(REGION), None, ALU.mult))
            link(dve.scalar_tensor_tensor(ta[:, :], tx[:, :], float(P), ta[:, :], ALU.mult, ALU.add))
            link(dve.tensor_scalar(row0[:, :], ta[:, :], float(E * REGION), None, ALU.min))
            link(dve.tensor_scalar(texp[:, :], te[:, :], float(E - 1), None, ALU.min))

            def copy_meta(j, u):
                dve.wait_ge(xs_in[u], 16 * (j // 2 + 1) if isinstance(j, int) else (j - u) * 8 + 16)
                if not (isinstance(j, int) and j < 2):
                    dve.wait_ge(added[u], 16 * (j // 2) if isinstance(j, int) else (j - u) * 8)
                dve.tensor_copy(meta[:, u, :], xs[:, u, D:D + 2]).then_inc(meta_done, 1)

            def gate_h(j, u):
                dve.wait_ge(sil_done, j + 1)
                dve.wait_ge(h3_ready, j + 1)
                if not (isinstance(j, int) and j < 2):
                    dve.wait_ge(gT_ready, j - 1)
                dve.tensor_tensor(gat[:, u, :], ps_h3[u][:, :], sil, ALU.mult).then_inc(g_done, 1)

            def scale_y(j, u):
                dve.wait_ge(y2_ready, j + 1)
                dve.wait_ge(meta_done, j + 1)
                if not (isinstance(j, int) and j < 2):
                    dve.wait_ge(added[u], 16 * (j // 2) if isinstance(j, int) else (j - u) * 8)
                dve.tensor_scalar(ys[:, u, :], ps_y[:, 0:D], meta[:, u, 1:2], None, ALU.mult).then_inc(y2_read, 1)

            for j in range(NT):
                copy_meta(j, j % 2)
                if j > 0:
                    scale_y(j - 1, (j - 1) % 2)
                gate_h(j, j % 2)
            scale_y(NT - 1, (NT - 1) % 2)


def kernel(x, ctx_512, L0_ffn_gate_w, L0_ffn_w1, L0_ffn_w2, L0_ffn_w3):
    import numpy as np
    import concourse.bacc as bacc
    from concourse.bass_utils import run_bass_kernel_spmd

    x, c = np.asarray(x), np.asarray(ctx_512)
    gw, w1, w2, w3 = (np.asarray(a) for a in (L0_ffn_gate_w, L0_ffn_w1, L0_ffn_w2, L0_ffn_w3))

    def up(w):
        return w.reshape(E, F, KC, P).transpose(3, 0, 2, 1).reshape(P, E * KC * F)

    cf, ci = constants()
    arrays = {
        "x": x.reshape(T, D),
        "kT": c.reshape(B, P, KV, HD).transpose(0, 3, 2, 1).reshape(P, KV * P),
        "v": c.reshape(T, KV * HD),
        "gateT": gw.reshape(E, KC, P).transpose(2, 1, 0),
        "w1T": up(w1),
        "w3T": up(w3),
        "w2T": w2.reshape(E, D, FC, P).transpose(3, 0, 2, 1).reshape(P, E * FC * D),
        "cf": cf,
        "ci": ci,
    }
    arrays = {f"in_{n}": np.ascontiguousarray(a) for n, a in arrays.items()}
    nc = bacc.Bacc("TRN2", target_bir_lowering=False, num_devices=1)
    args = [nc.dram_tensor(n, a.shape, mybir.dt.from_np(a.dtype), kind="ExternalInput").ap()
            for n, a in arrays.items()]
    out = nc.dram_tensor("out_rows", (T + P, D), F32, kind="ExternalOutput").ap()
    build(nc, *args, out)
    r = run_bass_kernel_spmd(nc, [arrays], core_ids=[0])
    return r.results[0]["out_rows"][:T].reshape(B, P, D)
```

```python
from contextlib import ExitStack

import concourse.bass as bass
from concourse import mybir
from concourse.bass import IndirectOffsetOnAxis

ALU = mybir.AluOpType
ACT = mybir.ActivationFunctionType
AX = mybir.AxisListType
F32 = mybir.dt.float32
BF16 = mybir.dt.bfloat16
F32R = mybir.dt.float32r
I32 = mybir.dt.int32
U32 = mybir.dt.uint32

P = 128
B, D, KV, G, HD = 16, 256, 8, 4, 8
H = KV * G
T = B * P
E, F, TOPK = 8, 512, 2
KC, FC = D // P, F // P
EPS = 1e-5
SCALE = 1.0 / float(HD) ** 0.5

TERMS = [(0, 0), (0, 1), (0, 2), (1, 0), (1, 1), (2, 0)]
QK_ROWS = len(TERMS) * HD
QKM_ROWS = QK_ROWS + 3
VW = HD + 1
OT = KV * VW

REGION = T + P
RW = D + 2
NT = (TOPK * T + E * (P - 1)) // P

C_ID, C_TRI, C_ONE, C_IOTA, C_BASE, C_TILE, C_END = 0, 128, 256, 384, 392, 400, 400 + NT


def constants():
    import numpy as np
    c = np.zeros((P, C_END), np.float32)
    p = np.arange(P)
    c[:, C_ID:C_ID + P] = np.eye(P)
    c[:, C_TRI:C_TRI + P] = p[:, None] < p[None, :]
    c[:, C_ONE:C_ONE + P] = 1.0
    c[:, C_IOTA:C_IOTA + E] = np.arange(E)
    c[:, C_BASE:C_BASE + E] = np.arange(E) * REGION
    c[:, C_TILE:C_TILE + NT] = np.arange(NT)
    i = (np.arange(B + 1)[None, :] * P + p[:, None]).astype(np.int32)
    return c, i


def build(nc, x, kT, v, gateT, w1T, w3T, w2T, cf, ci, out):
    kparts_d = nc.dram_tensor("kparts_d", (3, P, KV * P), BF16, kind="Internal").ap()
    qparts_d = nc.dram_tensor("qparts_d", (B, 3, D, P), BF16, kind="Internal").ap()
    slots_d = nc.dram_tensor("slots_d", (E * REGION + P, RW), F32, kind="Internal").ap()

    with ExitStack() as ctx:
        attention = ExitStack()

        def sb(name, shape, dt=F32):
            return ctx.enter_context(nc.sbuf_tensor(name, shape, dt))

        def sb1(name, shape, dt=F32):
            return attention.enter_context(nc.sbuf_tensor(name, shape, dt))

        def sem(name):
            return ctx.enter_context(nc.semaphore(name))

        def sems(name, n):
            return [sem(f"{name}{i}") for i in range(n)]

        w2 = sb("w2", [P, E * FC * D])
        gate = sb("gate", [P, KC, E])
        cst = sb("cst", [P, C_END])
        tok_id = sb("tok_id", [P, B + 1], I32)
        ident = cst[:, C_ID:C_ID + P]
        identb = sb("identb", [P, P], BF16)
        trib = sb("trib", [P, P], BF16)
        onesb = sb("onesb", [P, P], BF16)
        pad = sb("pad", [P, RW])
        cnti = sb("cnti", [P, 2, E], I32)
        ntl = sb("ntl", [P, E])
        cum = sb("cum", [P, E])
        ge = sb("ge", [P, NT, E])
        gn = sb("gn", [P, NT, E])
        te = sb("te", [P, NT])
        tx = sb("tx", [P, NT])
        ta = sb("ta", [P, NT])
        row0 = sb("row0", [P, NT], I32)
        texp = sb("texp", [P, NT], I32)
        dst = sb("dst", [P, E], I32)

        w13 = sb1("w13", [P, 2, E * KC * F])
        kst = sb1("kst", [64, B, KV * P], BF16)
        arena = sb1("arena", [P, 3 * H * P // 2])
        prob = sb1("prob", [P, 4, G * P])
        qst = arena[:, :].bitcast(BF16).rearrange("p (r h s) -> p r h s", r=3, h=H)
        kin = arena[:, 0:1024]
        kres = arena[:, 1024:2048]
        kp = arena[:, 2048:2048 + 1536].bitcast(BF16).rearrange("p (j n) -> p j n", j=3)
        vnat = sb1("vnat", [P, B, KV, HD])
        vblk = sb1("vblk", [P, 2, KV * (OT + VW)])
        xin = sb1("xin", [P, 2, D])
        xn1 = sb1("xn1", [P, 2, D])
        qp = sb1("qp", [P, 2, 3, D], BF16)
        qres = sb1("qres", [P, 2, D])
        oT = sb1("oT", [OT, 2, G * P])
        negm = sb1("negm", [P, 2, H])
        negp = sb1("negp", [P, 2, 3, H], BF16)
        negr = sb1("negr", [P, 2, H])
        negT = sb1("negT", [3 * H, 2, P], BF16)
        rden = sb1("rden", [P, H])
        att = sb1("att", [P, 2, D])
        xres = sb1("xres", [P, 2, D])
        x2 = sb1("x2", [P, 2, D])
        stat = sb1("stat", [P, 2, 8])
        mv = sb1("mv", [P, 2, 2])
        rs = sb1("rs", [P, 2, 6])
        rows = sb1("rows", [P, 2, TOPK, RW])
        xn2T = sb1("xn2T", [P, 2, KC, P])
        lg = sb1("lg", [P, E])
        top = sb1("top", [P, 8])
        topi = sb1("topi", [P, 8], U32)
        topf = sb1("topf", [P, TOPK])
        hot = sb1("hot", [P, 2, TOPK, E])
        hotb = sb1("hotb", [P, 2, E], BF16)
        seen = sb1("seen", [P, 2, E], BF16)
        dlt = sb1("dlt", [P, 4])
        pos = sb1("pos", [P, E])
        posk = sb1("posk", [P, TOPK, E])
        slot = sb1("slot", [P, 2, TOPK], I32)
        attention.close()

        wlo = sb("wlo", [P, 2, E * KC * F], F32R)
        whi = sb("whi", [P, 2, E * KC * F], F32R)
        xs = sb("xs", [P, 2, RW])
        xhi = sb("xhi", [P, 2, D], F32R)
        xlo = sb("xlo", [P, 2, D], F32R)
        sil = sb("sil", [P, F])[:, :]
        gat = sb("gat", [P, 2, F])
        gT = sb("gT", [P, FC, P])[:, :, :]
        ys = sb("ys", [P, 2, D])
        meta = sb("meta", [P, 2, 2])

        bank = [ctx.enter_context(nc.psum_tensor(f"bank{i}", [P, 512], F32)) for i in range(8)]
        ps_s = (bank[0], bank[1], bank[5])
        ps_e = bank[2:4]
        ps_o = bank[4]
        ps_a, ps_b = bank[6], bank[7]
        ps_h1, ps_h3 = bank[0:2], bank[2:4]
        ps_g, ps_y, ps_x = bank[4], bank[5], bank[6]

        in_id, in_small, in_k, in_v = sem("in_id"), sem("in_small"), sem("in_k"), sem("in_v")
        in_w13, in_w2 = sems("in_w13", 2), sem("in_w2")
        in_x, in_res = sems("in_x", 2), sems("in_res", 2)
        kparts_out, kst_in = sems("kparts_out", 3), sem("kst_in")
        qparts_out, qst_in = sems("qparts_out", 2), sems("qst_in", 3)
        neg_in = sems("neg_in", 3)
        x2_out, rows_out = sems("x2_out", 2), sems("rows_out", 2)
        pad_row, pads_out = sem("pad_row"), sem("pads_out")
        const_b, k_split = sem("const_b"), sem("k_split")
        v_zero, v_ready = sem("v_zero"), sem("v_ready")
        ln1, ln2, root1, root2 = sem("ln1"), sem("ln2"), sem("root1"), sem("root2")
        norm1, norm2, q_last = sem("norm1"), sem("norm2"), sem("q_last")
        qT_ready, q_part, q_res = sem("qT_ready"), sem("q_part"), sem("q_res")
        s_ready, max_done = sem("s_ready"), sem("max_done")
        neg_step, negT_ready, negT_read = sem("neg_step"), sem("negT_ready"), sem("negT_read")
        e_ready, exp_done, pv_done = sem("e_ready"), sem("exp_done"), sem("pv_done")
        oT_read, y_ready, y_step = sem("oT_read"), sem("y_ready"), sem("y_step")
        x2_ready, row_copied, tok_put = sem("x2_ready"), sem("row_copied"), sem("tok_put")
        xT2_ready, xT2_read, lg_ready, route = sem("xT2_ready"), sem("xT2_read"), sem("lg_ready"), sem("route")
        w_exp, w_step, hot_done = sem("w_exp"), sem("w_step"), sem("hot_done")
        seen_ready, rank_ready, pos_step = sem("seen_ready"), sem("rank_ready"), sem("pos_step")
        cnt_ready, table = sem("cnt_ready"), sem("table")
        xs_in = sems("xs_in", 2)
        hi_done, lo_done = sem("hi_done"), sem("lo_done")
        xT_ready, xhi_done, xlo_done = sem("xT_ready"), sem("xhi_done"), sem("xlo_done")
        h1_ready, h3_ready = sem("h1_ready"), sem("h3_ready")
        sil_done, g_done, gT_ready, gT_read = sem("sil_done"), sem("g_done"), sem("gT_ready"), sem("gT_read")
        y2_ready, y2_read, meta_done, added = sem("y2_ready"), sem("y2_read"), sem("meta_done"), sems("added", 2)

        LN, ROOT, ROUTE, POS, DST, TABLE = 4, 9, 6, 3, 1, 14

        W_PIECES = 8
        SPLIT = 512
        N_SPLIT = 2 * E * KC * F // SPLIT
        SPLITS = {i: [i - 1] for i in range(1, B - 2)}
        SPLITS.update({B - 2: [13, 20, 21], B - 1: [14, 22, 23, 24],
                       B: [15, 25, 26, 27], B + 1: [16, 17, 18, 19, 28, 29, 30, 31]})

        def split_column(m):
            return m // (N_SPLIT // 2), (m % (N_SPLIT // 2)) * SPLIT

        def tile_loop(engine, tile):
            for j in range(3):
                tile(j, j % 2)
            with engine.Fori(0, (NT - 5) // 2) as h:
                tile(h * 2 + 3, 1)
                tile(h * 2 + 4, 0)
            for j in range(NT - 2, NT):
                tile(j, j % 2)

        def known_below(j, n):
            return isinstance(j, int) and j < n

        def pair_count(j, u):
            return (j - u) * 8

        def pad_experts(engine, first):
            engine.wait_ge(table, DST)
            for e in range(first, E, 2):
                r = engine.value_load(dst[0:1, e:e + 1], min_val=e * REGION, max_val=e * REGION + T)
                engine.dma_start(slots_d[bass.ds(r, P), :], pad[:, :]).then_inc(pads_out, 16)

        block = ctx.enter_context(nc.Block())

        @block.sync
        def _(sp):
            for b in range(2):
                sp.dma_start(xin[:, b, :], x[b * P:(b + 1) * P, :]).then_inc(in_x[b], 16)
            sp.wait_ge(const_b, 1)
            for j in range(3):
                sp.dma_start(kst[QK_ROWS + j:QK_ROWS + j + 1, :, :], onesb[:, :]).then_inc(kst_in, 16)
            sp.dma_start(tok_id[:, :], ci).then_inc(in_small, 16)
            sp.dma_start(gate[:, :, :], gateT).then_inc(in_small, 16)
            for j, steps in enumerate((1, 3, 4)):
                sp.wait_ge(k_split, steps)
                sp.dma_start(kparts_d[j], kp[:, j, :]).then_inc(kparts_out[j], 16)

            def stack_k(part):
                sp.wait_ge(kparts_out[part], 16)
                kd = kparts_d.rearrange("j (b d) n -> j d b n", d=HD)
                for i, (_, j) in enumerate(TERMS):
                    if j == part:
                        sp.dma_start(kst[i * HD:(i + 1) * HD, :, :], kd[j]).then_inc(kst_in, 16)

            def load_x(b):
                sp.wait_ge(norm1, b - 1)
                sp.dma_start(xin[:, b % 2, :], x[b * P:(b + 1) * P, :]).then_inc(in_x[b % 2], 16)

            def load_res(b):
                if b >= 2:
                    sp.wait_ge(x2_ready, b - 1)
                sp.dma_start(xres[:, b % 2, :], x[b * P:(b + 1) * P, :]).then_inc(in_res[b % 2], 16)

            def store_x2(b):
                sp.wait_ge(x2_ready, b + 1)
                sp.dma_start(out[b * P:(b + 1) * P, :], x2[:, b % 2, :]).then_inc(x2_out[b % 2], 16)

            def write_q(b):
                sp.wait_ge(q_last, b + 1)
                sp.dma_start(qparts_d[b].rearrange("j (c p) s -> p j c s", c=KC),
                             qp[:, b % 2].rearrange("p j (c s) -> p j c s", c=KC))\
                    .then_inc(qparts_out[b % 2], 16)

            def stack_q(b):
                sp.wait_ge(qparts_out[b % 2], 16 * (b // 2 + 1))
                if b >= 3:
                    sp.wait_ge(e_ready, 8 * (b - 2))
                if b == 0:
                    for j in range(3):
                        sp.wait_ge(kparts_out[j], 16)
                qd = qparts_d[b].rearrange("j (h d) s -> j d h s", d=HD)
                for i, (j, _) in enumerate(TERMS):
                    sp.dma_start(qst[i * HD:(i + 1) * HD, b % 3, :, :], qd[j]).then_inc(qst_in[b % 3], 16)

            def lay_neg(b):
                sp.wait_ge(negT_read, b + 1)
                if b >= 3:
                    sp.wait_ge(e_ready, 8 * (b - 2))
                sp.dma_start(qst[QK_ROWS:QKM_ROWS, b % 3, :, :],
                             negT[:, b % 2, :]).then_inc(neg_in[b % 3], 16)

            def load_w13(n):
                w, c = n // W_PIECES, n % W_PIECES * (E * KC * F // W_PIECES)
                if n >= 2:
                    sp.wait_ge(in_w13[n % 2], 16 * (n // 2))
                sp.dma_start(w13[:, w, c:c + E * KC * F // W_PIECES],
                             (w1T, w3T)[w][:, c:c + E * KC * F // W_PIECES]).then_inc(in_w13[n % 2], 16)

            def load_w2(n):
                c = n * (E * FC * D // W_PIECES)
                sp.dma_start(w2[:, c:c + E * FC * D // W_PIECES], w2T[:, c:c + E * FC * D // W_PIECES])\
                    .then_inc(in_w2, 16)

            load_x(2)
            stack_k(0)
            write_q(0)
            stack_k(1)
            stack_k(2)
            for i in range(-2, B + 1):
                if 0 <= i + 2 < B:
                    stack_q(i + 2)
                if i + 5 < B:
                    load_x(i + 5)
                if i == -1:
                    sp.dma_start(vnat[:, :, :, :], v.rearrange("(b t) (k d) -> t b k d", t=P, k=KV))\
                        .then_inc(in_v, 16)
                if 0 <= i < B:
                    load_res(i)
                    load_w13(i)
                if 0 <= i + 1 < B:
                    lay_neg(i + 1)
                if 0 <= i + 3 < B:
                    write_q(i + 3)
                if 0 <= i - 1 < B:
                    store_x2(i - 1)
                if 0 <= i < W_PIECES:
                    load_w2(i)

            sp.wait_ge(pad_row, 3)
            sp.dma_start(out[T:T + P, :], pad[:, 0:D]).then_inc(pads_out, 16)
            sp.dma_start(slots_d[E * REGION:E * REGION + P, :], pad[:, :]).then_inc(pads_out, 16)
            pad_experts(sp, 0)
            sp.wait_ge(table, TABLE)

            def load_tile(j, u):
                r = sp.value_load(row0[0:1, bass.ds(j, 1)], min_val=0, max_val=E * REGION)
                if known_below(j, 1):
                    sp.wait_ge(pads_out, 16 * (E + 2))
                    for v_ in range(2):
                        sp.wait_ge(rows_out[v_], 16 * B)
                        sp.wait_ge(x2_out[v_], 16 * B // 2)
                if not known_below(j, 2):
                    sp.wait_ge(xT_ready, j - 1)
                    sp.wait_ge(meta_done, j - 1)
                sp.dma_start(xs[:, u, :], slots_d[bass.ds(r, P), :]).then_inc(xs_in[u], 16)

            tile_loop(sp, load_tile)

        @block.gpsimd
        def _(pool):
            pool.memset(vblk[:, :, :], 0.0).then_inc(v_zero, 1)
            pool.memset(seen[:, 0, :], 0.0).then_inc(seen_ready, 1)
            pool.wait_ge(v_zero, 1)
            vb = vblk[:, :, :].rearrange("p u (k r) -> p u k r", k=KV)
            for u in range(2):
                pool.memset(vb[:, u, :, HD:HD + 1], 1.0).then_inc(v_zero, 1)
            pool.memset(pad[:, :], 0.0).then_inc(pad_row, 1)
            def put_v(b):
                if b == 0:
                    pool.wait_ge(in_v, 16)
                if b >= 2:
                    pool.wait_ge(pv_done, 8 * (b - 1))
                pool.tensor_copy(vb[:, b % 2, :, 0:HD], vnat[:, b]).then_inc(v_ready, 1)

            def add_res(b):
                pool.wait_ge(y_step, 2 * b + 2)
                pool.wait_ge(in_res[b % 2], 16 * (b // 2 + 1))
                if b >= 2:
                    pool.wait_ge(x2_out[b % 2], 16 * (b // 2))
                    pool.wait_ge(norm2, b - 1)
                pool.tensor_tensor(x2[:, b % 2, :], att[:, b % 2, :], xres[:, b % 2, :], ALU.add)\
                    .then_inc(x2_ready, 1)

            def put_token(b):
                if b >= 2:
                    pool.wait_ge(rows_out[b % 2], 32 * (b // 2))
                for k in range(TOPK):
                    pool.tensor_copy(rows[:, b % 2, k, D:D + 1].bitcast(I32), tok_id[:, b:b + 1])\
                        .then_inc(tok_put, 1)

            def add_seen(b):
                pool.wait_ge(route, ROUTE * b + 6)
                pool.wait_ge(seen_ready, b + 1)
                if b >= 1:
                    pool.wait_ge(rank_ready, b)
                pool.tensor_tensor(seen[:, (b + 1) % 2, :], seen[:, b % 2, :], hotb[:, b % 2, :], ALU.add)\
                    .then_inc(seen_ready, 1)

            def scatter(b):
                pool.wait_ge(pos_step, POS * b + 3)
                pool.wait_ge(row_copied, b + 1)
                pool.wait_ge(w_step, 3 * b + 3)
                pool.wait_ge(tok_put, 2 * b + 2)
                for k in range(TOPK):
                    pool.indirect_dma_start(
                        slots_d, IndirectOffsetOnAxis(ap=slot[:, b % 2, k:k + 1], axis=0),
                        rows[:, b % 2, k, :], None).then_inc(rows_out[b % 2], 16)

            def root(n, b, guessed, done):
                v, y, h, p = (rs[:, n, c:c + 1] for c in range(4))
                pool.wait_ge(guessed, LN * b + 4)
                for r in (0, 4):
                    pool.tensor_scalar(h, y, y, v, ALU.mult, ALU.mult).then_inc(done, 1)
                    pool.wait_ge(done, ROOT * b + r + 1)
                    pool.tensor_scalar(p, h, 3 / 8, -10 / 8, ALU.mult, ALU.add).then_inc(done, 1)
                    pool.wait_ge(done, ROOT * b + r + 2)
                    pool.tensor_scalar(p, p, h, 15 / 8, ALU.mult, ALU.add).then_inc(done, 1)
                    pool.wait_ge(done, ROOT * b + r + 3)
                    pool.tensor_tensor(y, y, p, ALU.mult).then_inc(done, 1)
                    pool.wait_ge(done, ROOT * b + r + 4)
                pool.tensor_scalar(rs[:, n, 4:5], mv[:, n, 0:1], y, -1.0, ALU.mult, ALU.mult).then_inc(done, 1)

            def q_residual2(b):
                pool.wait_ge(q_part, 2 * b + 2)
                if b >= 2:
                    pool.wait_ge(qparts_out[b % 2], 16 * (b // 2))
                pool.tensor_tensor(qp[:, b % 2, 2, :], qres[:, b % 2, :], qp[:, b % 2, 1, :], ALU.subtract)\
                    .then_inc(q_last, 1)

            root(0, 0, ln1, root1)
            pool.wait_ge(pad_row, 1)
            pool.wait_ge(in_small, 32)
            pool.tensor_copy(pad[:, D:D + 1].bitcast(I32), tok_id[:, B:B + 1]).then_inc(pad_row, 2)
            pool.wait_ge(v_zero, 3)
            for i in range(-3, 0):
                q_residual2(i + 3)
                root(0, i + 4, ln1, root1)
            put_v(0)
            for i in range(B + 2):
                if i + 1 < B:
                    put_v(i + 1)
                if i - 3 >= 0:
                    scatter(i - 3)
                if i + 4 < B:
                    root(0, i + 4, ln1, root1)
                if 0 <= i - 1 < B:
                    add_res(i - 1)
                if i + 3 < B:
                    q_residual2(i + 3)
                if 0 <= i - 1 < B:
                    root(1, i - 1, ln2, root2)
                    put_token(i - 1)
                if 0 <= i - 2 < B - 1:
                    add_seen(i - 2)
            scatter(B - 1)

            pool.wait_ge(pads_out, 16 * (E + 2))
            for u in range(2):
                pool.wait_ge(x2_out[u], 16 * B // 2)

            def add_out(j, u):
                pool.wait_ge(y2_read, j + 1)
                pool.wait_ge(meta_done, j + 1)
                pool.indirect_dma_start(
                    out, IndirectOffsetOnAxis(ap=meta[:, u, 0:1].bitcast(I32), axis=0),
                    ys[:, u, :], None, compute_op=ALU.add).then_inc(added[u], 16)
                pool.wait_ge(added[u], pair_count(j, u) + 16)

            for j in range(NT):
                add_out(j, j % 2)

        @block.tensor
        def _(pe):
            pe.wait_ge(in_id, 16)

            def q_transpose(b):
                pe.wait_ge(norm1, b + 1)
                if b >= 6:
                    pe.wait_ge(pos_step, POS * (b - 6) + 1)
                elif b >= 3:
                    pe.wait_ge(negT_read, b - 2)
                elif b >= 1:
                    pe.wait_ge(q_res, b)
                for c in range(KC):
                    m = pe.transpose(ps_a[:, c * P:(c + 1) * P], xn1[:, b % 2, c * P:(c + 1) * P], ident)
                m.then_inc(qT_ready, 1)

            def score_group(b, g):
                if g == 0:
                    pe.wait_ge(qst_in[b % 3], 16 * len(TERMS) * (b // 3 + 1))
                    if b == 0:
                        pe.wait_ge(kst_in, 16 * (len(TERMS) + 3))
                n = 8 * b + g
                if n >= 3:
                    pe.wait_ge(max_done, n - 2)
                for h in range(G * g, G * g + G):
                    m = pe.matmul(ps_s[n % 3][:, (h % G) * P:(h % G + 1) * P], qst[0:QK_ROWS, b % 3, h, :],
                                  kst[0:QK_ROWS, b, g * P:(g + 1) * P], start=True, stop=True)
                m.then_inc(s_ready, 1)

            def neg_transpose(b):
                pe.wait_ge(neg_step, 4 * b + 4)
                if b == 0:
                    pe.wait_ge(const_b, 3)
                if b + 2 < B:
                    pe.wait_ge(q_res, b + 3)
                else:
                    pe.wait_ge(pos_step, POS * (b - 4) + 1)
                pe.transpose(ps_a[0:3 * H, 0:P // 2].bitcast(BF16), negp[:, b % 2].rearrange("p j h -> p (j h)"),
                             identb[:, :]).then_inc(negT_ready, 1)

            def e_products(b, k):
                if k == 0:
                    pe.wait_ge(neg_in[b % 3], 16 * (b // 3 + 1))
                if 8 * b + k >= 2:
                    pe.wait_ge(exp_done, 8 * b + k - 1)
                pe.matmul(ps_e[k % 2][:, :], kst[0:QKM_ROWS, b, k * P:(k + 1) * P],
                          qst[0:QKM_ROWS, b % 3, k * G:(k + 1) * G, :].rearrange("p h s -> p (h s)"),
                          start=True, stop=True).then_inc(e_ready, 1)

            def pv(b, k):
                if k == 0:
                    pe.wait_ge(v_ready, b + 1)
                    if b >= 1:
                        pe.wait_ge(oT_read, b)
                pe.wait_ge(exp_done, 8 * b + k + 1)
                pe.matmul(ps_o[0:OT, :], vblk[:, b % 2, k * OT:(k + 1) * OT], prob[:, k % 4, :],
                          start=(k == 0), stop=(k == KV - 1)).then_inc(pv_done, 1)

            def y_transpose(b):
                pe.wait_ge(oT_read, b + 1)
                if b >= 1:
                    pe.wait_ge(route, ROUTE * (b - 1 - (b == B - 1)) + 1)
                for g in range(G):
                    m = pe.transpose(ps_b[:, g * OT:(g + 1) * OT], oT[:, b % 2, g * P:(g + 1) * P],
                                     ident[0:OT, 0:OT])
                m.then_inc(y_ready, 1)

            def x2_transpose(b):
                pe.wait_ge(norm2, b + 1)
                pe.wait_ge(y_step, 2 * B if b == B - 2 else 2 * b + 2)
                if b == B - 1:
                    pe.wait_ge(route, ROUTE * (b - 1) + 1)
                for c in range(KC):
                    m = pe.transpose(ps_b[:, c * P:(c + 1) * P], rows[:, b % 2, 0, c * P:(c + 1) * P], ident)
                m.then_inc(xT2_ready, 1)

            def logits(b):
                pe.wait_ge(xT2_read, b + 1)
                if b == 0:
                    pe.wait_ge(in_small, 32)
                for c in range(KC):
                    m = pe.matmul(ps_b[:, 0:E], xn2T[:, b % 2, c, :], gate[:, c, :],
                                  start=(c == 0), stop=(c == KC - 1))
                m.then_inc(lg_ready, 1)

            def ranks(b):
                pe.wait_ge(route, ROUTE * b + 6)
                pe.wait_ge(seen_ready, b + 1)
                if b + 3 < B:
                    pe.wait_ge(negT_read, b + 4)
                else:
                    pe.wait_ge(pos_step, POS * (b - 1) + 1)
                pe.matmul(ps_a[:, 0:E], trib[:, :], hotb[:, b % 2, :], start=True, stop=False)
                pe.matmul(ps_a[:, 0:E], onesb[:, :], seen[:, b % 2, :], start=False, stop=True)\
                    .then_inc(rank_ready, 1)

            for i in range(-3, B + 2):
                for k in range(KV):
                    if 0 <= i < B:
                        e_products(i, k)
                    if k == 0 and 0 <= i - 1 < B:
                        pv(i - 1, KV - 1)
                    if k == 0 and i == B:
                        y_transpose(B - 1)
                    if k == 1 and 0 <= i + 3 < B:
                        q_transpose(i + 3)
                    if k < 4 and 0 <= i + 1 < B:
                        score_group(i + 1, k + 4)
                    if k >= 4 and 0 <= i + 2 < B:
                        score_group(i + 2, k - 4)
                    if k == 5 and 0 <= i + 1 < B:
                        neg_transpose(i + 1)
                    if k == 6 and 0 <= i - 2 < B:
                        ranks(i - 2)
                    if k >= 1 and 0 <= i < B:
                        pv(i, k - 1)
                    if k == 1 and 0 <= i - 2 < B:
                        x2_transpose(i - 2)
                    if k == 2 and 0 <= i - 2 < B:
                        logits(i - 2)
                    if k == 3 and 0 <= i - 1 < B - 1:
                        y_transpose(i - 1)
            pe.matmul(ps_b[:, 0:E], onesb[:, :], seen[:, (B - 1) % 2, :], start=True, stop=False)
            pe.matmul(ps_b[:, 0:E], onesb[:, :], hotb[:, (B - 1) % 2, :], start=False, stop=True)\
                .then_inc(cnt_ready, 1)

            pe.wait_ge(table, TABLE)
            pe.wait_ge(in_w2, 16 * W_PIECES)
            pe.wait_ge(lo_done, N_SPLIT)

            def tile_transpose(j, u):
                pe.wait_ge(xs_in[u], pair_count(j, u) + 16)
                if not known_below(j, 1):
                    pe.wait_ge(xhi_done, j)
                    pe.wait_ge(xlo_done, j)
                for c in range(KC):
                    m = pe.transpose(ps_x[:, c * P:(c + 1) * P], xs[:, u, c * P:(c + 1) * P], ident)
                m.then_inc(xT_ready, 1)

            def tile_h(j, u, w, e, bank_, done, used):
                pe.wait_ge(xhi_done, j + 1)
                if not known_below(j, 2):
                    pe.wait_ge(used, j - 1)
                for x_, w_ in ((xhi, whi), (xhi, wlo), (xlo, whi)):
                    if x_ is xlo:
                        pe.wait_ge(xlo_done, j + 1)
                    for c in range(KC):
                        m = pe.matmul(bank_[u][:, :], x_[:, u, c * P:(c + 1) * P],
                                      w_[:, w, bass.ds(e * (KC * F) + c * F, F)],
                                      start=(w_ is whi and x_ is xhi and c == 0), stop=(x_ is xlo and c == KC - 1))
                m.then_inc(done, 1)

            def g_transpose(j, u):
                pe.wait_ge(g_done, j + 1)
                if not known_below(j, 1):
                    pe.wait_ge(gT_read, j)
                for c in range(FC):
                    m = pe.transpose(ps_g[:, c * P:(c + 1) * P], gat[:, u, c * P:(c + 1) * P], ident)
                m.then_inc(gT_ready, 1)

            def tile_y(j, u, e):
                pe.wait_ge(gT_read, j + 1)
                if not known_below(j, 1):
                    pe.wait_ge(y2_read, j)
                for c in range(FC):
                    m = pe.matmul(ps_y[:, 0:D], gT[:, c, :], w2[:, bass.ds(e * (FC * D) + c * D, D)],
                                  start=(c == 0), stop=(c == FC - 1))
                m.then_inc(y2_ready, 1)

            def expert(j):
                return pe.value_load(texp[0:1, bass.ds(j, 1)], min_val=0, max_val=E - 1)

            def tile(j, u):
                e = expert(j)
                tile_h(j, u, 0, e, ps_h1, h1_ready, sil_done)
                if not known_below(j, 1):
                    g_transpose(j - 1, 1 - u)
                tile_h(j, u, 1, e, ps_h3, h3_ready, g_done)
                if not (isinstance(j, int) and j == NT - 1):
                    tile_transpose(j + 1, 1 - u)
                if not known_below(j, 1):
                    tile_y(j - 1, 1 - u, expert(j - 1))

            tile_transpose(0, 0)
            tile_loop(pe, tile)
            g_transpose(NT - 1, (NT - 1) % 2)
            tile_y(NT - 1, (NT - 1) % 2, expert(NT - 1))

        @block.scalar
        def _(act):
            act.dma_start(kin, kT).then_inc(in_k, 16)
            act.dma_start(cst[:, :], cf).then_inc(in_id, 16)
            act.wait_ge(in_k, 16)
            act.activation(kp[:, 0, :], kin, ACT.Copy).then_inc(k_split, 1)
            act.wait_ge(k_split, 2)
            act.activation(kp[:, 1, :], kres, ACT.Copy).then_inc(k_split, 1)

            def exps(b, k):
                n = 8 * b + k
                act.wait_ge(e_ready, n + 1)
                if n >= 4:
                    act.wait_ge(pv_done, n - 3)
                act.activation(prob[:, k % 4, :], ps_e[k % 2][:, :], ACT.Exp, scale=SCALE).then_inc(exp_done, 1)

            def q_part1(b):
                act.wait_ge(qT_ready, b + 1)
                if b >= 2:
                    act.wait_ge(qparts_out[b % 2], 16 * (b // 2))
                act.activation(qp[:, b % 2, 0, :], ps_a[:, 0:D], ACT.Copy).then_inc(q_part, 1)

            def q_part2(b):
                act.wait_ge(q_res, b + 1)
                act.activation(qp[:, b % 2, 1, :], qres[:, b % 2, :], ACT.Copy).then_inc(q_part, 1)

            def copy_oT(b):
                act.wait_ge(pv_done, 8 * b + 8)
                if b >= 2:
                    act.wait_ge(y_ready, b - 1)
                act.activation(oT[:, b % 2, :], ps_o[0:OT, :], ACT.Copy).then_inc(oT_read, 1)

            def copy_x2T(b):
                act.wait_ge(xT2_ready, b + 1)
                if b >= 2:
                    act.wait_ge(lg_ready, b - 1)
                act.activation(xn2T[:, b % 2].rearrange("p c s -> p (c s)"), ps_b[:, 0:D], ACT.Copy)\
                    .then_inc(xT2_read, 1)

            def copy_negT(b):
                act.wait_ge(negT_ready, b + 1)
                if b >= 2:
                    act.wait_ge(neg_in[(b - 2) % 3], 16 * ((b - 2) // 3 + 1))
                act.activation(negT[:, b % 2, :], ps_a[0:3 * H, 0:P // 2].bitcast(BF16), ACT.Copy)\
                    .then_inc(negT_read, 1)

            def copy_row(b):
                act.wait_ge(norm2, b + 1)
                act.activation(rows[:, b % 2, 1, 0:D], rows[:, b % 2, 0, 0:D], ACT.Copy).then_inc(row_copied, 1)

            def split_hi(m):
                w, c = split_column(m)
                piece, r = m // 2, (m % 16) // 4
                act.wait_ge(in_w13[piece % 2], 16 * (piece // 2 + 1))
                if w == 0:
                    act.wait_ge(e_ready, 8 * (m + 1))
                elif r < 3:
                    act.wait_ge(e_ready, 8 * (max(b for b in range(B) if b % 3 == r) + 1))
                else:
                    act.wait_ge(pv_done, 8 * B)
                act.activation(whi[:, w, c:c + SPLIT], w13[:, w, c:c + SPLIT], ACT.Copy).then_inc(hi_done, 1)

            def normal1(b):
                act.wait_ge(root1, ROOT * (b + 1))
                if b >= 2:
                    act.wait_ge(qT_ready, b - 1)
                act.activation(xn1[:, b % 2, :], xin[:, b % 2, :], ACT.Identity, scale=rs[:, 0, 1:2],
                               bias=rs[:, 0, 4:5]).then_inc(norm1, 1)

            def normal2(b):
                act.wait_ge(root2, ROOT * (b + 1))
                if b >= 2:
                    act.wait_ge(rows_out[b % 2], 32 * (b // 2))
                    act.wait_ge(xT2_ready, b - 1)
                act.activation(rows[:, b % 2, 0, 0:D], x2[:, b % 2, :], ACT.Identity, scale=rs[:, 1, 1:2],
                               bias=rs[:, 1, 4:5]).then_inc(norm2, 1)

            def weight_exp(b):
                act.wait_ge(route, ROUTE * b + 3)
                if b >= 1:
                    act.wait_ge(w_step, 3 * b)
                act.activation(dlt[:, 1:2], dlt[:, 0:1], ACT.Exp).then_inc(w_exp, 1)

            normal1(0)
            for i in range(-3, B + 2):
                todo = list(SPLITS.get(i, []))
                for k in range(KV):
                    if 0 <= i < B:
                        exps(i, k)
                    if todo and k >= 3 and i <= B:
                        split_hi(todo.pop(0))
                    if k == 0 and 0 <= i - 1 < B:
                        copy_oT(i - 1)
                    if k == 0 and 0 <= i - 2 < B:
                        normal2(i - 2)
                    if k == 1 and 0 <= i + 3 < B:
                        q_part1(i + 3)
                    if k == 1 and 0 <= i - 2 < B:
                        copy_x2T(i - 2)
                    if k == 2 and 0 <= i - 2 < B:
                        copy_row(i - 2)
                    if k == 3 and 0 <= i + 3 < B:
                        q_part2(i + 3)
                    if k == 5 and 0 <= i + 1 < B:
                        copy_negT(i + 1)
                    if k == 6 and 0 <= i - 2 < B:
                        weight_exp(i - 2)
                    if k == 7 and 0 <= i + 4 < B:
                        normal1(i + 4)
                for m in todo:
                    split_hi(m)

            def copy_xhi(j, u):
                act.wait_ge(xT_ready, j + 1)
                if not known_below(j, 2):
                    act.wait_ge(h3_ready, j - 1)
                act.activation(xhi[:, u, :], ps_x[:, 0:D], ACT.Copy).then_inc(xhi_done, 1)

            def silu(j, u):
                act.wait_ge(h1_ready, j + 1)
                if not known_below(j, 1):
                    act.wait_ge(g_done, j)
                act.activation(sil, ps_h1[u][:, :], ACT.Silu).then_inc(sil_done, 1)

            def copy_gT(j):
                act.wait_ge(gT_ready, j + 1)
                if not known_below(j, 1):
                    act.wait_ge(y2_ready, j)
                act.activation(gT.rearrange("p c s -> p (c s)"), ps_g[:, :], ACT.Copy).then_inc(gT_read, 1)

            def tile(j, u):
                silu(j, u)
                if not known_below(j, 1):
                    copy_gT(j - 1)
                if not (isinstance(j, int) and j == NT - 1):
                    copy_xhi(j + 1, 1 - u)

            pad_experts(act, 1)
            act.wait_ge(table, TABLE)
            copy_xhi(0, 0)
            tile_loop(act, tile)
            copy_gT(NT - 1)
            act.wait_ge(added[0], 16 * ((NT + 1) // 2))
            act.wait_ge(added[1], 16 * (NT // 2))

        @block.vector
        def _(dve):
            def stat_step(k, src, n, b, done):
                if k > 0:
                    dve.wait_ge(done, LN * b + k)
                if k == 0:
                    dve.bn_stats(stat[:, n, 0:6], src).then_inc(done, 1)
                elif k == 1:
                    dve.bn_aggr(mv[:, n, :], stat[:, n, 0:6]).then_inc(done, 1)
                elif k == 2:
                    dve.tensor_scalar(rs[:, n, 0:1], mv[:, n, 1:2], EPS, None, ALU.add).then_inc(done, 1)
                else:
                    dve.tensor_scalar(rs[:, n, 1:2].bitcast(I32), rs[:, n, 0:1].bitcast(I32), -0.5,
                                      float(0x5F3759DF), ALU.mult, ALU.add).then_inc(done, 1)

            def stat1(b, k):
                if k == 0:
                    dve.wait_ge(in_x[b % 2], 16 * (b // 2 + 1))
                    if b >= 1:
                        dve.wait_ge(norm1, b)
                stat_step(k, xin[:, b % 2, :], 0, b, ln1)

            def stat2(b, k):
                if k == 0:
                    dve.wait_ge(x2_ready, b + 1)
                    if b >= 1:
                        dve.wait_ge(norm2, b)
                stat_step(k, x2[:, b % 2, :], 1, b, ln2)

            def q_residual1(b):
                dve.wait_ge(q_part, 2 * b + 1)
                if b >= 2:
                    dve.wait_ge(q_last, b - 1)
                dve.tensor_tensor(qres[:, b % 2, :], ps_a[:, 0:D], qp[:, b % 2, 0, :], ALU.subtract)\
                    .then_inc(q_res, 1)

            def maxima(b, g):
                dve.wait_ge(s_ready, 8 * b + g + 1)
                dve.tensor_reduce(negm[:, b % 2, g * G:(g + 1) * G],
                                  ps_s[(8 * b + g) % 3][:, :].rearrange("p (h t) -> p h t", h=G), AX.X, ALU.max,
                                  negate=True).then_inc(max_done, 1)

            def neg_split(b, k):
                m, r, q = negm[:, b % 2, :], negr[:, b % 2, :], negp[:, b % 2]
                if k == 0:
                    dve.wait_ge(max_done, 8 * b + 8)
                    if b >= 2:
                        dve.wait_ge(negT_ready, b - 1)
                    dve.tensor_copy(q[:, 0, :], m).then_inc(neg_step, 1)
                    return
                dve.wait_ge(neg_step, 4 * b + k)
                if k == 1:
                    dve.tensor_tensor(r, m, q[:, 0, :], ALU.subtract).then_inc(neg_step, 1)
                elif k == 2:
                    dve.tensor_copy(q[:, 1, :], r).then_inc(neg_step, 1)
                else:
                    dve.tensor_tensor(q[:, 2, :], r, q[:, 1, :], ALU.subtract).then_inc(neg_step, 1)

            def normalise(b, k):
                y = ps_b[:, 0:G * OT].rearrange("p (g k c) -> p g k c", g=G, k=KV)
                r = rden[:, :].rearrange("p (g k) -> p g k", g=G)
                if k == 0:
                    dve.wait_ge(y_ready, b + 1)
                    dve.reciprocal(r, y[:, :, :, HD]).then_inc(y_step, 1)
                    return
                dve.wait_ge(y_step, 2 * b + 1)
                if b >= 2:
                    dve.wait_ge(x2_ready, b - 1)
                dve.tensor_tensor(att[:, b % 2, :].rearrange("p (k g d) -> p g k d", g=G, d=HD),
                                  y[:, :, :, 0:HD], r[:, :, :, None].broadcast_to((P, G, KV, HD)), ALU.mult)\
                    .then_inc(y_step, 1)

            def read_logits(b):
                dve.wait_ge(lg_ready, b + 1)
                dve.tensor_copy(lg[:, :], ps_b[:, 0:E]).then_inc(route, 1)

            def choose(b, k):
                n = ROUTE * b
                if k != 3:
                    dve.wait_ge(route, n + k)
                if k == 1:
                    dve.max(top[:, :], lg[:, :]).then_inc(route, 1)
                elif k == 2:
                    if b >= 1:
                        dve.wait_ge(w_exp, b)
                    dve.tensor_tensor(dlt[:, 0:1], top[:, 1:2], top[:, 0:1], ALU.subtract).then_inc(route, 1)
                elif k == 3:
                    dve.max_index(topi[:, :], top[:, :], lg[:, :]).then_inc(route, 1)
                elif k == 4:
                    dve.tensor_copy(topf[:, :], topi[:, 0:TOPK]).then_inc(route, 1)
                elif k == 5:
                    if b >= 2:
                        dve.wait_ge(seen_ready, b)
                        dve.wait_ge(rank_ready, b - 1)
                    dve.tensor_tensor(hot[:, b % 2], cst[:, None, C_IOTA:C_IOTA + E].broadcast_to((P, TOPK, E)),
                                      topf[:, :, None].broadcast_to((P, TOPK, E)), ALU.is_equal)\
                        .then_inc(hot_done, 1)
                    return

            def both_choices(b):
                dve.wait_ge(hot_done, b + 1)
                dve.tensor_tensor(hotb[:, b % 2, :], hot[:, b % 2, 0, :], hot[:, b % 2, 1, :], ALU.add)\
                    .then_inc(route, 1)

            def split_lo(i, first=0, last=N_SPLIT):
                done = first + sum(len(SPLITS.get(e, [])) for e in range(i))
                for n, m in enumerate(SPLITS.get(i, [])[first:last]):
                    w, c = split_column(m)
                    dve.wait_ge(hi_done, done + n + 1)
                    dve.tensor_tensor(wlo[:, w, c:c + SPLIT], w13[:, w, c:c + SPLIT],
                                      whi[:, w, c:c + SPLIT], ALU.subtract).then_inc(lo_done, 1)

            def weigh(b, k):
                if k == 0:
                    dve.wait_ge(w_exp, b + 1)
                    if b >= 2:
                        dve.wait_ge(rows_out[b % 2], 32 * (b // 2))
                    dve.tensor_scalar(dlt[:, 2:3], dlt[:, 1:2], 1.0, None, ALU.add).then_inc(w_step, 1)
                    return
                dve.wait_ge(w_step, 3 * b + k)
                if k == 1:
                    dve.reciprocal(rows[:, b % 2, 0, D + 1:D + 2], dlt[:, 2:3]).then_inc(w_step, 1)
                else:
                    dve.tensor_tensor(rows[:, b % 2, 1, D + 1:D + 2], dlt[:, 1:2], rows[:, b % 2, 0, D + 1:D + 2],
                                      ALU.mult).then_inc(w_step, 1)

            def pad_rows():
                dve.wait_ge(cnt_ready, 1)
                dve.tensor_tensor(dst[:, :], ps_b[:, 0:E], cst[:, C_BASE:C_BASE + E], ALU.add).then_inc(table, DST)

            def place(b, k):
                n = POS * b
                if k == 0:
                    dve.wait_ge(rank_ready, b + 1)
                    dve.tensor_tensor(pos[:, :], ps_a[:, 0:E], cst[:, C_BASE:C_BASE + E], ALU.add)\
                        .then_inc(pos_step, 1)
                    return
                dve.wait_ge(pos_step, n + k)
                if k == 1:
                    dve.tensor_tensor(posk[:, :, :], hot[:, b % 2], pos[:, None, :].broadcast_to((P, TOPK, E)),
                                      ALU.mult).then_inc(pos_step, 1)
                    return
                if b >= 2:
                    dve.wait_ge(rows_out[b % 2], 32 * (b // 2))
                with nc.allow_low_precision(reason="slot numbers are whole and below 2**24"):
                    dve.tensor_reduce(slot[:, b % 2, :], posk[:, :, :], AX.X, ALU.add).then_inc(pos_step, 1)

            dve.memset(onesb[:, :], 1.0).then_inc(const_b, 1)
            for k in range(4):
                stat1(0, k)
            dve.wait_ge(k_split, 1)
            dve.tensor_tensor(kres, kin, kp[:, 0, :], ALU.subtract).then_inc(k_split, 1)
            dve.wait_ge(k_split, 3)
            dve.tensor_tensor(kp[:, 2, :], kres, kp[:, 1, :], ALU.subtract).then_inc(k_split, 1)
            dve.wait_ge(in_id, 16)
            dve.tensor_copy(identb[:, :], ident).then_inc(const_b, 1)
            dve.tensor_copy(trib[:, :], cst[:, C_TRI:C_TRI + P]).then_inc(const_b, 1)
            for i in range(-3, B + 3):
                if 0 <= i + 1 < B:
                    maxima(i + 1, 4)
                if 0 <= i + 4 < B:
                    stat1(i + 4, 0)
                if 0 <= i + 1 < B:
                    maxima(i + 1, 5)
                if 0 <= i + 4 < B:
                    stat1(i + 4, 1)
                if 0 <= i + 3 < B:
                    q_residual1(i + 3)
                if 0 <= i + 4 < B:
                    stat1(i + 4, 2)
                if B <= i <= B + 1:
                    split_lo(i - 1)
                if i == B:
                    normalise(B - 1, 0)
                    normalise(B - 1, 1)
                    stat2(B - 1, 0)
                    stat2(B - 1, 1)
                    stat2(B - 1, 2)
                    stat2(B - 1, 3)
                if 0 <= i - 2 < B:
                    read_logits(i - 2)
                if 0 <= i + 4 < B:
                    stat1(i + 4, 3)
                if 0 <= i + 1 < B:
                    maxima(i + 1, 6)
                if i < B:
                    split_lo(i - 1)
                if 0 <= i + 1 < B:
                    maxima(i + 1, 7)
                if 0 <= i - 1 < B - 1:
                    normalise(i - 1, 0)
                if 0 <= i + 1 < B:
                    neg_split(i + 1, 0)
                if 0 <= i - 1 < B - 1:
                    normalise(i - 1, 1)
                if 0 <= i + 1 < B:
                    neg_split(i + 1, 1)
                if 0 <= i - 2 < B:
                    choose(i - 2, 1)
                if 0 <= i + 1 < B:
                    neg_split(i + 1, 2)
                if 0 <= i - 2 < B:
                    choose(i - 2, 2)
                    choose(i - 2, 3)
                if 0 <= i + 1 < B:
                    neg_split(i + 1, 3)
                if 0 <= i - 2 < B:
                    choose(i - 2, 4)
                if 0 <= i + 2 < B:
                    maxima(i + 2, 0)
                if 0 <= i - 2 < B:
                    choose(i - 2, 5)
                if 0 <= i - 1 < B - 1:
                    stat2(i - 1, 0)
                if 0 <= i - 2 < B:
                    both_choices(i - 2)
                if i - 2 == B - 1:
                    pad_rows()
                if 0 <= i - 1 < B - 1:
                    stat2(i - 1, 1)
                if 0 <= i + 2 < B:
                    maxima(i + 2, 1)
                if 0 <= i - 1 < B - 1:
                    stat2(i - 1, 2)
                if 0 <= i + 2 < B:
                    maxima(i + 2, 2)
                if 0 <= i - 1 < B - 1:
                    stat2(i - 1, 3)
                if 0 <= i - 2 < B:
                    place(i - 2, 0)
                    weigh(i - 2, 0)
                    place(i - 2, 1)
                    weigh(i - 2, 1)
                    place(i - 2, 2)
                    weigh(i - 2, 2)
                if 0 <= i + 2 < B:
                    maxima(i + 2, 3)

            step = [DST]

            def link(ins):
                step[0] += 1
                ins.then_inc(table, 1)
                dve.wait_ge(table, step[0])

            bc = (P, NT, E)
            link(dve.tensor_scalar(cnti[:, 0, :], ps_b[:, 0:E], float(P - 1), None, ALU.add))
            link(dve.tensor_scalar(cnti[:, 1, :], cnti[:, 0, :], 7, None, ALU.arith_shift_right))
            link(dve.tensor_copy(ntl[:, :], cnti[:, 1, :]))
            link(dve.tensor_tensor_scan(cum[:, :], cst[:, C_ONE:C_ONE + E], ntl[:, :], 0.0, ALU.mult, ALU.add))
            tiles = cst[:, C_TILE:C_TILE + NT]
            link(dve.tensor_tensor(ge[:, :, :], tiles[:, :, None].broadcast_to(bc),
                                   cum[:, None, :].broadcast_to(bc), ALU.is_ge))
            link(dve.tensor_tensor(gn[:, :, :], ge[:, :, :], ntl[:, None, :].broadcast_to(bc), ALU.mult))
            link(dve.tensor_reduce(te[:, :], ge[:, :, :], AX.X, ALU.add))
            link(dve.tensor_reduce(tx[:, :], gn[:, :, :], AX.X, ALU.add))
            link(dve.tensor_tensor(tx[:, :], tiles, tx[:, :], ALU.subtract))
            link(dve.tensor_scalar(ta[:, :], te[:, :], float(REGION), None, ALU.mult))
            link(dve.scalar_tensor_tensor(ta[:, :], tx[:, :], float(P), ta[:, :], ALU.mult, ALU.add))
            link(dve.tensor_scalar(row0[:, :], ta[:, :], float(E * REGION), None, ALU.min))
            link(dve.tensor_scalar(texp[:, :], te[:, :], float(E - 1), None, ALU.min))

            split_lo(B + 1)

            def copy_meta(j, u):
                dve.wait_ge(xs_in[u], pair_count(j, u) + 16)
                if not known_below(j, 2):
                    dve.wait_ge(added[u], pair_count(j, u))
                dve.tensor_copy(meta[:, u, :], xs[:, u, D:D + 2]).then_inc(meta_done, 1)

            def gate_h(j, u):
                dve.wait_ge(sil_done, j + 1)
                dve.wait_ge(h3_ready, j + 1)
                if not known_below(j, 2):
                    dve.wait_ge(gT_ready, j - 1)
                dve.tensor_tensor(gat[:, u, :], ps_h3[u][:, :], sil, ALU.mult).then_inc(g_done, 1)

            def scale_y(j, u):
                dve.wait_ge(y2_ready, j + 1)
                dve.wait_ge(meta_done, j + 1)
                if not known_below(j, 2):
                    dve.wait_ge(added[u], pair_count(j, u))
                dve.tensor_scalar(ys[:, u, :], ps_y[:, 0:D], meta[:, u, 1:2], None, ALU.mult).then_inc(y2_read, 1)

            def copy_xlo(j, u):
                dve.wait_ge(xhi_done, j + 1)
                if not known_below(j, 2):
                    dve.wait_ge(h3_ready, j - 1)
                dve.tensor_tensor(xlo[:, u, :], ps_x[:, 0:D], xhi[:, u, :], ALU.subtract).then_inc(xlo_done, 1)

            def tile(j, u):
                copy_meta(j, u)
                gate_h(j, u)
                if not (isinstance(j, int) and j == NT - 1):
                    copy_xlo(j + 1, 1 - u)
                if not known_below(j, 1):
                    scale_y(j - 1, 1 - u)

            copy_xlo(0, 0)
            tile_loop(dve, tile)
            scale_y(NT - 1, (NT - 1) % 2)


def kernel(x, ctx_512, L0_ffn_gate_w, L0_ffn_w1, L0_ffn_w2, L0_ffn_w3):
    import numpy as np
    import concourse.bacc as bacc
    from concourse.bass_utils import run_bass_kernel_spmd

    x, c = np.asarray(x), np.asarray(ctx_512)
    gw, w1, w2, w3 = (np.asarray(a) for a in (L0_ffn_gate_w, L0_ffn_w1, L0_ffn_w2, L0_ffn_w3))

    def up(w):
        return w.reshape(E, F, KC, P).transpose(3, 0, 2, 1).reshape(P, E * KC * F)

    cf, ci = constants()
    arrays = {
        "x": x.reshape(T, D),
        "kT": c.reshape(B, P, KV, HD).transpose(0, 3, 2, 1).reshape(P, KV * P),
        "v": c.reshape(T, KV * HD),
        "gateT": gw.reshape(E, KC, P).transpose(2, 1, 0),
        "w1T": up(w1),
        "w3T": up(w3),
        "w2T": w2.reshape(E, D, FC, P).transpose(3, 0, 2, 1).reshape(P, E * FC * D),
        "cf": cf,
        "ci": ci,
    }
    arrays = {f"in_{n}": np.ascontiguousarray(a) for n, a in arrays.items()}
    nc = bacc.Bacc("TRN2", target_bir_lowering=False, num_devices=1)
    args = [nc.dram_tensor(n, a.shape, mybir.dt.from_np(a.dtype), kind="ExternalInput").ap()
            for n, a in arrays.items()]
    out = nc.dram_tensor("out_rows", (T + P, D), F32, kind="ExternalOutput").ap()
    build(nc, *args, out)
    r = run_bass_kernel_spmd(nc, [arrays], core_ids=[0])
    return r.results[0]["out_rows"][:T].reshape(B, P, D)
```
